# Optimizing a Trainium2 kernel written in Bass

```python
import numpy as np
import jax
import jax.numpy as jnp

def _softmax(x, axis=-1):
    return jax.nn.softmax(x, axis=axis)

def _gelu(x):
    return jax.nn.gelu(x, approximate=True)

def _silu(x):
    return jax.nn.silu(x)

def _sigmoid(x):
    return jax.nn.sigmoid(x)

def _layernorm(x, axis=-1, eps=1e-05):
    m = jnp.mean(x, axis=axis, keepdims=True)
    v = jnp.var(x, axis=axis, keepdims=True)
    return (x - m) / jnp.sqrt(v + eps)

def _scatter_add(tgt, idx, src, axis=0):
    return tgt.at[idx].add(src)

def _segment_sum(src, seg, n):
    return jax.ops.segment_sum(src, seg, n)
kernel_name = 'mk_macaron_d1_jaxref_r2_1cf9a4'

def setup_inputs(seed: int=0):
    np.random.seed(seed)
    _w = jnp.asarray

    def _L0_attn_setup():
        import jax, jax.numpy as jnp
        import numpy as np
        B_, L_, D_ = (2, 512, 512)
        EXPAND, N_STATE, K_CONV = (2, 16, 4)
        D_INNER = D_ * EXPAND
        DT_RANK = (D_ + 15) // 16

        def _layernorm(x, w, b, eps=1e-05):
            mu = jnp.mean(x, axis=-1, keepdims=True)
            var = jnp.mean(jnp.square(x - mu), axis=-1, keepdims=True)
            return (x - mu) * jax.lax.rsqrt(var + eps) * w + b
        key = jax.random.key(seed)
        ks = jax.random.split(key, 10)
        sc = 0.02
        x = jax.random.normal(ks[0], (B_, L_, D_), jnp.float32)
        ln_w = jnp.ones((D_,), jnp.float32)
        ln_b = jnp.zeros((D_,), jnp.float32)
        W_in = jax.random.normal(ks[1], (2 * D_INNER, D_), jnp.float32) * sc
        W_conv = jax.random.normal(ks[2], (D_INNER, K_CONV), jnp.float32) * 0.2
        b_conv = jnp.zeros((D_INNER,), jnp.float32)
        W_xproj = jax.random.normal(ks[3], (DT_RANK + 2 * N_STATE, D_INNER), jnp.float32) * sc
        W_dt = jax.random.normal(ks[4], (D_INNER, DT_RANK), jnp.float32) * DT_RANK ** (-0.5)
        dt = jnp.exp(jax.random.uniform(ks[5], (D_INNER,), jnp.float32) * (np.log(0.1) - np.log(0.001)) + np.log(0.001))
        b_dt = dt + jnp.log(-jnp.expm1(-dt))
        A_log = jnp.log(jnp.broadcast_to(jnp.arange(1, N_STATE + 1, dtype=jnp.float32), (D_INNER, N_STATE)))
        D_skip = jnp.ones((D_INNER,), jnp.float32)
        W_out = jax.random.normal(ks[6], (D_, D_INNER), jnp.float32) * sc
        return {'x': x, 'ln_w': ln_w, 'ln_b': ln_b, 'W_in': W_in, 'W_conv': W_conv, 'b_conv': b_conv, 'W_xproj': W_xproj, 'W_dt': W_dt, 'b_dt': b_dt, 'A_log': A_log, 'D_skip': D_skip, 'W_out': W_out}
    _L0_attn_in = _L0_attn_setup()

    def _L0_ffn_setup():
        import jax, jax.numpy as jnp
        import numpy as np
        DIM = 512

        def _reference_tuple_inner(x, W_r, W_k, W_v, mu_r, mu_k):
            B, T, C = x.shape
            x_prev = jnp.concatenate([jnp.zeros((B, 1, C), x.dtype), x[:, :-1, :]], axis=1)
            xr = mu_r * x + (1.0 - mu_r) * x_prev
            xk = mu_k * x + (1.0 - mu_k) * x_prev
            r = jax.nn.sigmoid(jnp.einsum('btc,dc->btd', xr, W_r))
            k = jnp.einsum('btc,dc->btd', xk, W_k)
            k_act = jnp.square(jax.nn.relu(k))
            out = r * jnp.einsum('btc,dc->btd', k_act, W_v)
            new_state = x[:, -1, :]
            return (out, new_state)
        key = jax.random.key(seed)
        ks = jax.random.split(key, 6)
        B, T, C = (8, 1024, DIM)
        x = jax.random.normal(ks[0], (B, T, C), dtype=jnp.float32)
        s = 1.0 / np.sqrt(C)
        W_r = jax.random.uniform(ks[1], (C, C), jnp.float32, -s, s)
        W_k = jax.random.uniform(ks[2], (C, C), jnp.float32, -s, s)
        W_v = jax.random.uniform(ks[3], (C, C), jnp.float32, -s, s)
        mu_r = jax.random.uniform(ks[4], (C,), jnp.float32)
        mu_k = jax.random.uniform(ks[5], (C,), jnp.float32)
        return {'x': x, 'W_r': W_r, 'W_k': W_k, 'W_v': W_v, 'mu_r': mu_r, 'mu_k': mu_k}
    _L0_ffn_in = _L0_ffn_setup()
    _d = {'L0_attn_x': _L0_attn_in['x'], 'L0_attn_ln_w': _L0_attn_in['ln_w'], 'L0_attn_ln_b': _L0_attn_in['ln_b'], 'L0_attn_W_in': _L0_attn_in['W_in'], 'L0_attn_W_conv': _L0_attn_in['W_conv'], 'L0_attn_b_conv': _L0_attn_in['b_conv'], 'L0_attn_W_xproj': _L0_attn_in['W_xproj'], 'L0_attn_W_dt': _L0_attn_in['W_dt'], 'L0_attn_b_dt': _L0_attn_in['b_dt'], 'L0_attn_A_log': _L0_attn_in['A_log'], 'L0_attn_D_skip': _L0_attn_in['D_skip'], 'L0_attn_W_out': _L0_attn_in['W_out'], 'L0_ffn_W_r': _L0_ffn_in['W_r'], 'L0_ffn_W_k': _L0_ffn_in['W_k'], 'L0_ffn_W_v': _L0_ffn_in['W_v'], 'L0_ffn_mu_r': _L0_ffn_in['mu_r'], 'L0_ffn_mu_k': _L0_ffn_in['mu_k']}
    _x0 = _d['L0_attn_x']
    _d['L0_attn_x'] = jax.random.normal(jax.random.fold_in(jax.random.key(seed), 1), (4, 2048, 512), dtype=_x0.dtype)
    del _x0
    return _d

def reference(L0_attn_x, L0_attn_ln_w, L0_attn_ln_b, L0_attn_W_in, L0_attn_W_conv, L0_attn_b_conv, L0_attn_W_xproj, L0_attn_W_dt, L0_attn_b_dt, L0_attn_A_log, L0_attn_D_skip, L0_attn_W_out, L0_ffn_W_r, L0_ffn_W_k, L0_ffn_W_v, L0_ffn_mu_r, L0_ffn_mu_k):

    def _L0_attn_ref(x, ln_w, ln_b, W_in, W_conv, b_conv, W_xproj, W_dt, b_dt, A_log, D_skip, W_out):
        import jax, jax.numpy as jnp
        import numpy as np
        B_, L_, D_ = (2, 512, 512)
        EXPAND, N_STATE, K_CONV = (2, 16, 4)
        D_INNER = D_ * EXPAND
        DT_RANK = (D_ + 15) // 16

        def _layernorm(x, w, b, eps=1e-05):
            mu = jnp.mean(x, axis=-1, keepdims=True)
            var = jnp.mean(jnp.square(x - mu), axis=-1, keepdims=True)
            return (x - mu) * jax.lax.rsqrt(var + eps) * w + b
        B, L, D = x.shape
        residual = x
        xn = _layernorm(x, ln_w, ln_b)
        xz = jnp.einsum('bld,ed->ble', xn, W_in)
        xs, z = jnp.split(xz, 2, axis=-1)
        xp = jnp.pad(xs, ((0, 0), (K_CONV - 1, 0), (0, 0)))
        xc = b_conv + sum((xp[:, k:k + L, :] * W_conv[:, k] for k in range(K_CONV)))
        xc = jax.nn.silu(xc)
        dbl = jnp.einsum('ble,re->blr', xc, W_xproj)
        dt_low = dbl[..., :DT_RANK]
        B_ssm = dbl[..., DT_RANK:DT_RANK + N_STATE]
        C_ssm = dbl[..., DT_RANK + N_STATE:]
        delta = jax.nn.softplus(jnp.einsum('blr,er->ble', dt_low, W_dt) + b_dt)
        A = -jnp.exp(A_log)
        dA = jnp.exp(delta[..., None] * A)
        dBx = delta[..., None] * B_ssm[:, :, None, :] * xc[..., None]

        def step(h, inp):
            dA_t, dBx_t, C_t = inp
            h = dA_t * h + dBx_t
            y_t = jnp.einsum('bdn,bn->bd', h, C_t)
            return (h, y_t)
        h0 = jnp.zeros((B, D_INNER, N_STATE), x.dtype)
        _, ys = jax.lax.scan(step, h0, (dA.transpose(1, 0, 2, 3), dBx.transpose(1, 0, 2, 3), C_ssm.transpose(1, 0, 2)))
        y = ys.transpose(1, 0, 2) + D_skip * xc
        y = y * jax.nn.silu(z)
        out = jnp.einsum('ble,de->bld', y, W_out)
        return out + residual

    def _L0_ffn_ref(x, W_r, W_k, W_v, mu_r, mu_k):
        import jax, jax.numpy as jnp
        import numpy as np
        DIM = 512

        def _reference_tuple_inner(x, W_r, W_k, W_v, mu_r, mu_k):
            B, T, C = x.shape
            x_prev = jnp.concatenate([jnp.zeros((B, 1, C), x.dtype), x[:, :-1, :]], axis=1)
            xr = mu_r * x + (1.0 - mu_r) * x_prev
            xk = mu_k * x + (1.0 - mu_k) * x_prev
            r = jax.nn.sigmoid(jnp.einsum('btc,dc->btd', xr, W_r))
            k = jnp.einsum('btc,dc->btd', xk, W_k)
            k_act = jnp.square(jax.nn.relu(k))
            out = r * jnp.einsum('btc,dc->btd', k_act, W_v)
            new_state = x[:, -1, :]
            return (out, new_state)
        return _reference_tuple_inner(x, W_r, W_k, W_v, mu_r, mu_k)[0]
    x = L0_attn_x
    x = x + 0.5 * _L0_ffn_ref(_layernorm(x, axis=-1), L0_ffn_W_r, L0_ffn_W_k, L0_ffn_W_v, L0_ffn_mu_r, L0_ffn_mu_k)
    x = x + _L0_attn_ref(_layernorm(x, axis=-1), L0_attn_ln_w, L0_attn_ln_b, L0_attn_W_in, L0_attn_W_conv, L0_attn_b_conv, L0_attn_W_xproj, L0_attn_W_dt, L0_attn_b_dt, L0_attn_A_log, L0_attn_D_skip, L0_attn_W_out)
    x = x + 0.5 * _L0_ffn_ref(_layernorm(x, axis=-1), L0_ffn_W_r, L0_ffn_W_k, L0_ffn_W_v, L0_ffn_mu_r, L0_ffn_mu_k)
    return x

_drawn_inputs = setup_inputs


def setup_inputs(seed=0):
    import zlib

    import numpy as np

    out = dict(_drawn_inputs(seed))
    spreads = {'L0_attn_ln_w': (1.0, 0.2),
     'L0_attn_ln_b': (0.0, 0.1),
     'L0_attn_b_conv': (0.0, 0.1),
     'L0_attn_D_skip': (1.0, 0.2)}
    factors = {}
    for name, (base, spread) in spreads.items():
        noise = np.random.default_rng([zlib.crc32(name.encode()), seed]).standard_normal(out[name].shape)
        drawn = base * np.exp(spread * noise) if base else spread * noise
        out[name] = jnp.asarray(drawn.astype(out[name].dtype))
    for name, factor in factors.items():
        out[name] = (out[name] * factor).astype(out[name].dtype)
    return out
```

```python
from contextlib import ExitStack

import concourse.bass as bass
from concourse import mybir

ALU = mybir.AluOpType
ACT = mybir.ActivationFunctionType
F32 = mybir.dt.float32
I32 = mybir.dt.int32

P = 128
T = 128
SEG = T + 1
EPS = 1e-5
RSQRT_GUESS = 1597463007.0
NEWTON = 4


class Marks:

    def __init__(self, sem, names):
        self.sem, self.names = sem, names.split() if isinstance(names, str) else names
        assert len(set(self.names)) == len(self.names)

    def at(self, chunk, name):
        return chunk * len(self.names) + (self.names.index(name) + 1)


def due(value):
    return not isinstance(value, int) or value > 0


def build(nc, x, mu_r, mu_k, w_r, w_k, w_v, ln_w, ln_b, w_in, w_conv, b_conv, w_x, w_dt, b_dt,
          a_log, d_skip, w_out, out):
    BATCHES, L, D = x.shape
    E, NS = a_log.shape
    R = w_dt.shape[0]
    KC = w_conv.shape[1]
    B = 2
    PAIRS = BATCHES // B
    NCH = L // T * PAIRS
    W = B * T
    CT, ET = D // P, E // P
    HT = ET // 2
    TB = W // P
    NSTEP = 2 * NS
    XR = R + 2 * NS
    NEXP, NSTT = NSTEP * HT, NSTEP * TB
    DAB = 3
    NBG = 4
    assert TB == 2 and CT == 4 and HT == 4 and T == P and PAIRS == 2 and R == 32 and NS == 16 and XR == 64

    with ExitStack() as ctx:
        def sb(name, shape, dt=F32):
            return ctx.enter_context(nc.sbuf_tensor(name, shape, dt))

        def ps(name, shape):
            return ctx.enter_context(nc.psum_tensor(name, shape, F32))

        def sem(name):
            return ctx.enter_context(nc.semaphore(name))

        decay = ps("decay", [P, DAB, 512])
        h_rows = ps("h_rows", [P, TB, 512])
        mm = ps("mm", [P, 3, 512])

        wr_sb, wk_sb, wv_sb = (sb(n, [P, CT, D]) for n in ("wr_sb", "wk_sb", "wv_sb"))
        win_sb = sb("win_sb", [P, CT, 2 * E])
        wx_sb = sb("wx_sb", [P, ET, XR])
        wdt_sb = sb("wdt_sb", [P, E])
        wout_sb = sb("wout_sb", [P, ET, D])
        ident = sb("ident", [P, P])
        vec = sb("vec", [P, 6, CT])
        conv_sb = sb("conv_sb", [P, ET, KC])
        evec = sb("evec", [P, 4, ET])
        neg_a = sb("neg_a", [P, ET, NS])
        xscale = sb("xscale", [XR, 1])

        xin = sb("xin", [P, TB, D])
        res = sb("res", [P, TB, D])
        res_prev = sb("res_prev", [P, TB, D])
        xout = sb("xout", [P, TB, D])
        ffn_row = [sb(f"ffn_row{i}", [P, TB, D]) for i in range(2)]
        ffn_col = [sb(f"ffn_col{i}", [P, CT, B * SEG]) for i in range(2)]
        ffn_mix = [sb(f"ffn_mix{i}", [P, CT, W]) for i in range(2)]
        ffn_last = [sb(f"ffn_last{i}", [P, PAIRS, CT, B]) for i in range(2)]
        stats = [sb(f"stats{i}", [P, TB, 6]) for i in range(3)]
        mv = [sb(f"mv{i}", [P, TB, 2]) for i in range(3)]
        nv = [sb(f"nv{i}", [P, 2 * TB]) for i in range(3)]
        nt = [sb(f"nt{i}", [P, 2 * TB]) for i in range(3)]
        rs = [sb(f"rs{i}", [P, 2 * TB]) for i in range(3)]
        xn_col = sb("xn_col", [P, CT, W])
        xs_pad = sb("xs_pad", [P, 2, 2, B, T + KC - 1])
        xs_last = sb("xs_last", [P, PAIRS, ET, B, KC - 1])
        xc2 = sb("xc2", [P, ET, W])
        th = sb("th", [P, 2, 512])
        zth = sb("zth", [P, 2, 512])
        gate = sb("gate", [P, ET, W])
        xdbl = sb("xdbl", [P, W])
        c_next = sb("c_next", [P, TB, NS])
        c_now = sb("c_now", [P, TB, NS])
        delta = sb("delta", [P, 2, HT, W])
        u = sb("u", [P, 2, HT, W])
        b_all = sb("b_all", [P, 2, NBG, W])
        dbx = sb("dbx", [P, 2, HT, B, SEG])
        h = sb("h", [P, 2, HT, B, SEG])
        state = sb("state", [P, PAIRS, NSTEP, HT, B])
        y_rows = sb("y_rows", [P, 2, TB, 512])

        b_dram = nc.dram_tensor("b_scratch", (NCH, NS * W), F32).ap()

        w_loaded, v_loaded = sem("w_loaded"), sem("v_loaded")
        x_loaded, out_stored = sem("x_loaded"), sem("out_stored")
        b_stored = sem("b_stored")
        b_loaded = [sem("b_loaded0"), sem("b_loaded1")]
        init_pool, init_dve, init_act = sem("init_pool"), sem("init_dve"), sem("init_act")

        passed_sp, passed_dve, passed_pool = sem("passed_sp"), sem("passed_dve"), sem("passed_pool")

        decay_done = sem("decay_done")
        dbx_done = sem("dbx_done")
        scan_done = sem("scan_done")
        saved = sem("saved")
        h_turned = sem("h_turned")
        y_added = sem("y_added")
        res_kept = sem("res_kept")

        newton = ["guess"] + [f"{q}{i}" for i in range(NEWTON) for q in ("yy", "vyy", "half", "y")]
        f_pe = [Marks(sem(f"ffn{i}_pe"), "T0 T1 r0 r1 k0 k1 v0 v1") for i in range(2)]
        f_act = [Marks(sem(f"ffn{i}_act"), "xn0 xn1 lead last pr0 pr1 pr2 pr3 th0 th1 "
                       "pk0 pk1 pk2 pk3 rel0 sq0 rel1 sq1") for i in range(2)]
        f_dve = [Marks(sem(f"ffn{i}_dve"), "st0 st1 mv0 mv1 ln0 ln1 xr0 xr1 xr2 xr3 "
                       "xk0 xk1 xk2 xk3 g0 g1 o0 o1") for i in range(2)]
        f_pool = [Marks(sem(f"ffn{i}_pool"), ["v"] + newton) for i in range(2)]
        m_pe = Marks(sem("mamba_pe"), "T0 T1 xs0 xs1 xs2 xs3 xp")
        m_act = Marks(sem("mamba_act"), ["xn0", "xn1", "xn2", "xn3"] + [
            f"{q}{j}" for j in range(4) for q in ("raw", "lead", "last", "tapa", "tapb", "th")] + ["xp"])
        m_dve = Marks(sem("mamba_dve"), ["st0", "st1", "mv0", "mv1", "ln0", "ln1", "in0", "in1"] + [
            f"{q}{j}" for j in range(4) for q in ("c0a", "c0b", "c1a", "c1b", "c2a", "c2b", "silu")])
        m_pool = Marks(sem("mamba_pool"), ["v", "v2"] + newton + ["res"])
        h_pe = Marks(sem("half_pe"), "C dt0_0 dt0_1 sd0_0 sd0_1 dt1_0 dt1_1 sd1_0 sd1_1")
        h_act = Marks(sem("half_act"), ["C"] + [
            f"{q}{hf}" for hf in range(2)
            for q in ("xa", "xb", "xc", "xd", "abs", "exp", "ln", "da", "db", "dc", "dd", "ya", "yb")])
        h_dve = Marks(sem("half_dve"), "delta0 C delta1")
        h_pool = Marks(sem("half_pool"), "u0 u1")
        z_pe = Marks(sem("gate_pe"), "0 1 2 3")
        z_act = Marks(sem("gate_act"), "0 1 2 3")
        z_dve = Marks(sem("gate_dve"), "0 1 2 3")
        y_pe = Marks(sem("y_pe"), "T0 T1 T2 T3 o0 o1")
        y_dve = Marks(sem("y_dve"), "g0 g1 g2 g3 x0 x1")

        GROUPS = [("dt1_0", 0, h_act, "xb1"), ("dt1_1", 0, h_act, "xd1"),
                  ("YT2", -1, y_dve, "g2"), ("YT3", -1, y_dve, "g3"),
                  ("f0T0", 1, f_act[0], "xn0"), ("f0T1", 1, f_act[0], "xn1"),
                  ("o0", -1, y_dve, "x0"), ("sd1_0", 0, h_act, "ya1"), ("sd1_1", 0, h_act, "yb1"),
                  ("o1", -1, y_dve, "x1"),
                  ("f0r0", 1, f_act[0], "th0"), ("f0r1", 1, f_act[0], "th1"),
                  ("f0k0", 1, f_act[0], "rel0"), ("f0k1", 1, f_act[0], "rel1"),
                  ("f1T0", -1, f_act[1], "xn0"), ("f1T1", -1, f_act[1], "xn1"),
                  ("z0", 0, z_dve, "0"), ("z1", 0, z_dve, "1"),
                  ("f0v0", 1, f_dve[0], "g0"), ("f0v1", 1, f_dve[0], "g1"),
                  ("f1r0", -1, f_act[1], "th0"), ("f1r1", -1, f_act[1], "th1"),
                  ("z2", 0, z_dve, "2"), ("z3", 0, z_dve, "3"),
                  ("YT0", 0, y_dve, "g0"), ("YT1", 0, y_dve, "g1"),
                  ("mT0", 1, m_act, "xn1"), ("mT1", 1, m_act, "xn3"),
                  ("xs0", 1, m_act, "tapb0"), ("xs1", 1, m_act, "tapb1"),
                  ("xs2", 1, m_act, "tapb2"), ("xs3", 1, m_act, "tapb3"),
                  ("f1k0", -1, f_act[1], "rel0"), ("f1k1", -1, f_act[1], "rel1"),
                  ("f1v0", -1, f_dve[1], "g0"), ("f1v1", -1, f_dve[1], "g1"),
                  ("xp", 1, m_act, "xp"), ("C", 1, h_act, "C"),
                  ("dt0_0", 1, h_act, "xb0"), ("dt0_1", 1, h_act, "xd0"),
                  ("sd0_0", 1, h_act, "ya0"), ("sd0_1", 1, h_act, "yb0")]
        assert len(GROUPS) % 3 == 0
        NUMBER = {g[0]: n for n, g in enumerate(GROUPS)}

        def bank(group):
            return mm[:, NUMBER[group] % 3, :]

        def bank_free(it, group):
            n = NUMBER[group] - 3
            while True:
                if n < 0:
                    n, it = n + len(GROUPS), it - 1
                _, off, marks, name = GROUPS[n]
                if not isinstance(it, int) or 0 <= it + off < NCH:
                    return marks.sem, marks.at(it + off, name)
                if it < -1:
                    return None
                n -= 3

        def col3(t):
            return t.rearrange("p (b t) -> p b t", b=B)

        def fcol(i, ct, lo):
            return ffn_col[i][:, ct, :].rearrange("p (b s) -> p b s", b=B)[:, :, lo:lo + T]

        def run(body, eng):
            for it in (-1, 0, 1):
                body(it, it % PAIRS)
            with eng.Fori(1, NCH // PAIRS - 1) as turn:
                for pair in range(PAIRS):
                    body(turn * PAIRS + pair, pair)
            for it in (NCH - 2, NCH - 1, NCH):
                body(it, it % PAIRS)

        def has(it, off):
            return not isinstance(it, int) or 0 <= it + off < NCH

        block = ctx.enter_context(nc.Block())

        @block.sync
        def _(sp):
            def rows_of(dram, k, pair, tb):
                return dram[B * pair + tb, bass.ds((k - pair) * (T // PAIRS), T), :]

            def load_x(k, pair):
                if due(count := m_pool.at(k - 1, "res")):
                    sp.wait_ge(m_pool.sem, count)
                    sp.sem_inc(passed_sp, 1)
                if due(count := m_dve.at(k - 1, "in1")):
                    sp.wait_ge(m_dve.sem, count)
                    sp.sem_inc(passed_sp, 1)
                for tb in range(TB):
                    sp.dma_start(xin[:, tb, :], rows_of(x, k, pair, tb)).then_inc(x_loaded, 16)

            for i, v in ((0, mu_r), (1, mu_k), (4, ln_w), (5, ln_b)):
                sp.dma_start(vec[:, i, :], v).then_inc(v_loaded, 16)
            for i, v in ((0, b_conv), (1, b_dt), (2, d_skip)):
                sp.dma_start(evec[:, i, :], v).then_inc(v_loaded, 16)
            sp.dma_start(conv_sb[:, :, :], w_conv.rearrange("(t p) k -> p t k", p=P)).then_inc(v_loaded, 16)
            sp.dma_start(neg_a[:, :, :], a_log.rearrange("(t p) n -> p t n", p=P)).then_inc(v_loaded, 16)
            load_x(0, 0)
            for dst, src in ((wr_sb, w_r), (wk_sb, w_k), (wv_sb, w_v), (win_sb, w_in), (wx_sb, w_x)):
                sp.dma_start(dst[:, :, :], src.rearrange("(t p) n -> p t n", p=P)).then_inc(w_loaded, 16)
            sp.wait_ge(init_pool, 2)
            sp.dma_start(wdt_sb[0:R, :], w_dt).then_inc(w_loaded, 16)
            sp.dma_start(wout_sb[:, :, :], w_out.rearrange("(t p) n -> p t n", p=P)).then_inc(w_loaded, 16)

            def load_b(k, j):
                if j < 2:
                    if due(count := 16 * (k + 1)):
                        sp.wait_ge(b_stored, count)
                        sp.sem_inc(passed_sp, 1)
                if due(count := 2 * NSTEP * k + 2 * NBG * (j - 1)):
                    sp.wait_ge(dbx_done, count)
                    sp.sem_inc(passed_sp, 1)
                sp.dma_start(b_all[:, j % 2, :, :],
                             b_dram[bass.ds(k, 1), (j % 4) * NBG * W:(j % 4 + 1) * NBG * W]
                             .rearrange("o (n w) -> o n w", n=NBG).broadcast_to([P, NBG, W])
                             ).then_inc(b_loaded[j % 2], 16)

            def body(it, pair):
                if has(it, 0):
                    for j in range(2, 6):
                        load_b(it, j)
                if has(it, 1) and has(it, 2):
                    load_x(it + 2, pair)
                if has(it, 0):
                    for j in range(6, 8):
                        load_b(it, j)
                if has(it, -1):
                    for tb in range(TB):
                        if due(count := f_dve[1].at(it - 1, f"o{tb}")):
                            sp.wait_ge(f_dve[1].sem, count)
                            sp.sem_inc(passed_sp, 1)
                        sp.dma_start(rows_of(out, it - 1, (pair - 1) % PAIRS, tb),
                                     xout[:, tb, :]).then_inc(out_stored, 16)
                if has(it, 1):
                    sp.wait_ge(m_act.sem, m_act.at(it + 1, "xp"))
                    sp.sem_inc(passed_sp, 1)
                    sp.dma_start(b_dram[bass.ds(it + 1, 1), :].rearrange("o (n w) -> (o n) w", n=NS),
                                 xdbl[R:R + NS, :]).then_inc(b_stored, 16)
                    load_b(it + 1, 0)
                    load_b(it + 1, 1)

            run(body, sp)
            sp.wait_ge(out_stored, 16 * TB * NCH)

        @block.tensor
        def _(pe):
            pe.wait_ge(init_pool, 3)
            pe.wait_ge(w_loaded, 16 * 7)

            def turn_rows(it, i, group, src, marks, dst_chunk, names):
                for j in range(2):
                    if free := bank_free(it, group + f"T{j}"):
                        pe.wait_ge(*free)
                    o = bank(group + f"T{j}").rearrange("p (c w) -> p c w", c=2)
                    for c in range(2):
                        for tb in range(TB):
                            ct = 2 * j + c
                            last = pe.transpose(o[:, c, tb * P:(tb + 1) * P],
                                                src[:, tb, ct * P:(ct + 1) * P], ident[:, :])
                    last.then_inc(marks.sem, 1)

            def ffn_turn(it, i, k):
                pe.wait_ge(f_dve[i].sem, f_dve[i].at(k, "ln1"))
                turn_rows(it, i, f"f{i}", ffn_row[i], f_pe[i], k, None)

            def ffn_r(it, i, k, tb):
                pe.wait_ge(f_dve[i].sem, f_dve[i].at(k, "xr3"))
                if free := bank_free(it, f"f{i}r{tb}"):
                    pe.wait_ge(*free)
                for ct in range(CT):
                    last = pe.matmul(bank(f"f{i}r{tb}"), ffn_mix[i][:, ct, tb * P:(tb + 1) * P],
                                     wr_sb[:, ct, :], start=ct == 0, stop=ct == CT - 1)
                last.then_inc(f_pe[i].sem, 1)

            def ffn_k(it, i, k, j):
                pe.wait_ge(f_dve[i].sem, f_dve[i].at(k, "xk3"))
                if free := bank_free(it, f"f{i}k{j}"):
                    pe.wait_ge(*free)
                o = bank(f"f{i}k{j}").rearrange("p (c w) -> p c w", c=2)
                for c in range(2):
                    dt = 2 * j + c
                    for ct in range(CT):
                        last = pe.matmul(o[:, c, :], wk_sb[:, ct, dt * P:(dt + 1) * P],
                                         ffn_mix[i][:, ct, :], start=ct == 0, stop=ct == CT - 1)
                last.then_inc(f_pe[i].sem, 1)

            def ffn_v(it, i, k, tb):
                pe.wait_ge(f_act[i].sem, f_act[i].at(k, "sq1"))
                if free := bank_free(it, f"f{i}v{tb}"):
                    pe.wait_ge(*free)
                for ct in range(CT):
                    last = pe.matmul(bank(f"f{i}v{tb}"), ffn_col[i][:, ct, tb * P:(tb + 1) * P],
                                     wv_sb[:, ct, :], start=ct == 0, stop=ct == CT - 1)
                last.then_inc(f_pe[i].sem, 1)

            def mamba_turn(it, k):
                pe.wait_ge(m_dve.sem, m_dve.at(k, "in1"))
                turn_rows(it, 0, "m", ffn_row[0], m_pe, k, None)

            def project(it, group, e0, marks):
                if free := bank_free(it, group):
                    pe.wait_ge(*free)
                o = bank(group).rearrange("p (c w) -> p c w", c=2)
                for c in range(2):
                    for ct in range(CT):
                        last = pe.matmul(o[:, c, :], win_sb[:, ct, e0 + c * P:e0 + (c + 1) * P],
                                         xn_col[:, ct, :], start=ct == 0, stop=ct == CT - 1)
                last.then_inc(marks.sem, 1)

            def xs(it, k, j):
                pe.wait_ge(m_act.sem, m_act.at(k, "xn3"))
                project(it, f"xs{j}", 2 * j * P, m_pe)

            def z(it, j):
                project(it, f"z{j}", E + 2 * j * P, z_pe)

            def xproj(it, k):
                pe.wait_ge(m_dve.sem, m_dve.at(k, "silu3"))
                if free := bank_free(it, "xp"):
                    pe.wait_ge(*free)
                for et in range(ET):
                    last = pe.matmul(bank("xp")[0:XR, 0:W], wx_sb[:, et, :], xc2[:, et, :],
                                     start=et == 0, stop=et == ET - 1)
                last.then_inc(m_pe.sem, 1)

            def turn_c(it, k):
                pe.wait_ge(m_act.sem, m_act.at(k, "xp"))
                if free := bank_free(it, "C"):
                    pe.wait_ge(*free)
                for tb in range(TB):
                    last = pe.transpose(bank("C")[:, tb * P:(tb + 1) * P],
                                        xdbl[:, tb * P:(tb + 1) * P], ident[:, :])
                last.then_inc(h_pe.sem, 1)

            def dt_proj(it, hf, j):
                if free := bank_free(it, f"dt{hf}_{j}"):
                    pe.wait_ge(*free)
                o = bank(f"dt{hf}_{j}").rearrange("p (c w) -> p c w", c=2)
                for c in range(2):
                    et = HT * hf + 2 * j + c
                    last = pe.matmul(o[:, c, :], wdt_sb[:, et * P:(et + 1) * P], xdbl[:, :],
                                     start=True, stop=True)
                last.then_inc(h_pe.sem, 1)

            def turn_skip(it, k, hf, tb):
                pe.wait_ge(h_act.sem, h_act.at(k, f"dd{hf}"))
                if free := bank_free(it, f"sd{hf}_{tb}"):
                    pe.wait_ge(*free)
                for e in range(HT):
                    last = pe.transpose(bank(f"sd{hf}_{tb}")[:, e * P:(e + 1) * P],
                                        ffn_mix[1][:, e, tb * P:(tb + 1) * P], ident[:, :])
                last.then_inc(h_pe.sem, 1)

            def turn_y(it, k, j):
                hf = j // 2
                if due(count := NSTT * k + TB * NS * (hf + 1)):
                    pe.wait_ge(y_added, count)
                if free := bank_free(it, f"YT{j}"):
                    pe.wait_ge(*free)
                o = bank(f"YT{j}").rearrange("p (c w) -> p c w", c=2)
                for c in range(2):
                    e = 2 * (j % 2) + c
                    for tb in range(TB):
                        last = pe.transpose(o[:, c, tb * P:(tb + 1) * P],
                                            y_rows[:, hf, tb, e * P:(e + 1) * P], ident[:, :])
                last.then_inc(y_pe.sem, 1)

            def out_proj(it, k, tb, part):
                if part == 0:
                    pe.wait_ge(y_dve.sem, y_dve.at(k, "g3"))
                    if free := bank_free(it, f"o{tb}"):
                        pe.wait_ge(*free)
                for et in range(HT * part, HT * part + HT):
                    last = pe.matmul(bank(f"o{tb}"), gate[:, et, tb * P:(tb + 1) * P],
                                     wout_sb[:, et, :], start=et == 0, stop=et == ET - 1)
                if part == 1:
                    last.then_inc(y_pe.sem, 1)

            def turn_h(it, s, tb):
                if tb == 0:
                    if due(count := NEXP * it + HT * (s + 1)):
                        pe.wait_ge(scan_done, count)
                if due(count := NSTT * it + TB * (s - 1) + tb + 1):
                    pe.wait_ge(y_added, count)
                for e in range(HT):
                    last = pe.transpose(h_rows[:, tb, e * P:(e + 1) * P],
                                        h[:, s % 2, e, tb, 1:SEG], ident[:, :])
                last.then_inc(h_turned, 1)

            def body(it, pair):
                scan, front, back = has(it, 0), has(it, 1), has(it, -1)
                f, b = it + 1, it - 1
                for s in range(NSTEP):
                    if scan:
                        turn_h(it, s, 0)
                        turn_h(it, s, 1)
                    if scan:
                        if s == 0:
                            dt_proj(it, 1, 0)
                            dt_proj(it, 1, 1)
                        if s in (10, 11):
                            z(it, s - 10)
                        if s in (16, 17):
                            z(it, s - 14)
                    if back:
                        if s == 1:
                            turn_y(it, b, 2)
                            turn_y(it, b, 3)
                    if front and s == 1:
                        ffn_turn(it, 0, f)
                    if back and s in (2, 3):
                        out_proj(it, b, 0, s - 2)
                    if scan and s == 3:
                        turn_skip(it, it, 1, 0)
                        turn_skip(it, it, 1, 1)
                    if back and s in (4, 5):
                        out_proj(it, b, 1, s - 4)
                    if front:
                        if s in (6, 7):
                            ffn_r(it, 0, f, s - 6)
                        if s in (8, 9):
                            ffn_k(it, 0, f, s - 8)
                    if back and s == 9:
                        ffn_turn(it, 1, b)
                    if front and s in (12, 13):
                        ffn_v(it, 0, f, s - 12)
                    if back and s in (14, 15):
                        ffn_r(it, 1, b, s - 14)
                    if scan and s == 17:
                        turn_y(it, it, 0)
                        turn_y(it, it, 1)
                    if front:
                        if s == 18:
                            mamba_turn(it, f)
                        if 19 <= s < 23:
                            xs(it, f, s - 19)
                    if back:
                        if s in (23, 24):
                            ffn_k(it, 1, b, s - 23)
                        if s in (25, 26):
                            ffn_v(it, 1, b, s - 25)
                    if front:
                        if s == 27:
                            xproj(it, f)
                        if s == 28:
                            turn_c(it, f)
                        if s == 29:
                            dt_proj(it, 0, 0)
                            dt_proj(it, 0, 1)
                        if s == 31:
                            turn_skip(it, f, 0, 0)
                            turn_skip(it, f, 0, 1)

            run(body, pe)

        @block.scalar
        def _(act):
            act.wait_ge(v_loaded, 16 * 9)
            act.activation(neg_a[:, :, :], neg_a[:, :, :], ACT.Exp).then_inc(init_act, 1)
            act.wait_ge(init_act, 1)
            act.activation(neg_a[:, :, :], neg_a[:, :, :], ACT.Copy, scale=-1.0).then_inc(init_act, 1)
            act.wait_ge(init_act, 2)
            act.wait_ge(init_dve, 5)
            act.wait_ge(init_pool, 11)

            def ffn_columns(i, k, pair):
                if due(count := f_pe[i].at(k - 1, "v1")):
                    act.wait_ge(f_pe[i].sem, count)
                for j in range(2):
                    act.wait_ge(f_pe[i].sem, f_pe[i].at(k, f"T{j}"))
                    for_j = ffn_col[i][:, 2 * j:2 * j + 2, :].rearrange("p c (b s) -> p (c b) s", b=B)
                    act.activation(for_j[:, :, 1:SEG],
                                   bank(f"f{i}T{j}").rearrange("p (q t) -> p q t", t=T),
                                   ACT.Copy).then_inc(f_act[i].sem, 1)
                both = ffn_col[i][:, :, :].rearrange("p c (b s) -> p (c b) s", b=B)
                last = ffn_last[i][:, pair, :, :].rearrange("p c b -> p (c b)").unsqueeze(2)
                if due(count := f_act[i].at(k - 1, "last")):
                    act.wait_ge(f_act[i].sem, count)
                act.activation(both[:, :, 0:1], last, ACT.Copy).then_inc(f_act[i].sem, 1)
                act.wait_ge(f_act[i].sem, f_act[i].at(k, "lead"))
                act.activation(last, both[:, :, T:SEG], ACT.Copy).then_inc(f_act[i].sem, 1)

            def ffn_before(i, k, q, scanned=True):
                act.wait_ge(f_act[i].sem, f_act[i].at(k, "lead"))
                if q == 1:
                    act.wait_ge(f_pe[i].sem, f_pe[i].at(k, "r1"))
                elif i == 1:
                    act.wait_ge(h_pe.sem, h_pe.at(k + 1 if scanned else k, "sd1_1"))
                for ct in range(CT):
                    act.activation(col3(ffn_mix[i][:, ct, :]), fcol(i, ct, 0), ACT.Copy,
                                   scale=vec[:, 2 + q, ct:ct + 1]).then_inc(f_act[i].sem, 1)

            def ffn_tanh(i, k, tb):
                act.wait_ge(f_pe[i].sem, f_pe[i].at(k, f"r{tb}"))
                act.activation(ffn_row[i][:, tb, :], bank(f"f{i}r{tb}"), ACT.Tanh,
                               scale=0.5).then_inc(f_act[i].sem, 1)

            def ffn_relu2(i, k, j):
                act.wait_ge(f_pe[i].sem, f_pe[i].at(k, f"k{j}"))
                act.wait_ge(f_dve[i].sem, f_dve[i].at(k, "xk3"))
                o = ffn_col[i][:, 2 * j:2 * j + 2, 0:W]
                act.activation(o, bank(f"f{i}k{j}").rearrange("p (c w) -> p c w", c=2),
                               ACT.Relu).then_inc(f_act[i].sem, 1)
                act.wait_ge(f_act[i].sem, f_act[i].at(k, f"rel{j}"))
                act.activation(o, o, ACT.Square).then_inc(f_act[i].sem, 1)

            def mamba_columns(k):
                if due(count := z_pe.at(k - 1, "3")):
                    act.wait_ge(z_pe.sem, count)
                for ct in range(CT):
                    if ct % 2 == 0:
                        act.wait_ge(m_pe.sem, m_pe.at(k, f"T{ct // 2}"))
                    act.activation(xn_col[:, ct, :], bank(f"mT{ct // 2}")[:, (ct % 2) * W:(ct % 2 + 1) * W],
                                   ACT.Identity, scale=vec[:, 4, ct:ct + 1],
                                   bias=vec[:, 5, ct:ct + 1]).then_inc(m_act.sem, 1)

            def conv_start(k, j, pair):
                act.wait_ge(m_pe.sem, m_pe.at(k, f"xs{j}"))
                if j >= 2:
                    act.wait_ge(m_dve.sem, m_dve.at(k, f"c2b{j - 2}"))
                else:
                    if due(count := m_dve.at(k - 1, f"c2b{j + 2}")):
                        act.wait_ge(m_dve.sem, count)
                pad = xs_pad[:, j % 2, :, :, :].rearrange("p c b s -> p (c b) s")
                hist = xs_last[:, pair, 2 * j:2 * j + 2, :, :].rearrange("p c b s -> p (c b) s")
                src = bank(f"xs{j}")
                act.activation(pad[:, :, KC - 1:], src.rearrange("p (q t) -> p q t", t=T),
                               ACT.Copy).then_inc(m_act.sem, 1)
                if due(count := m_act.at(k - 1, f"last{j}")):
                    act.wait_ge(m_act.sem, count)
                act.activation(pad[:, :, 0:KC - 1], hist, ACT.Copy).then_inc(m_act.sem, 1)
                act.wait_ge(m_act.sem, m_act.at(k, f"lead{j}"))
                act.activation(hist, pad[:, :, T:T + KC - 1], ACT.Copy).then_inc(m_act.sem, 1)
                if due(count := h_pool.at(k - 1, "u1")):
                    act.wait_ge(h_pool.sem, count)
                if due(count := h_act.at(k - 1, "dd1")):
                    act.wait_ge(h_act.sem, count)
                for c in range(2):
                    et = 2 * j + c
                    act.activation(xc2[:, et, :], src[:, c * W:(c + 1) * W], ACT.Identity,
                                   scale=conv_sb[:, et, KC - 1:KC],
                                   bias=evec[:, 0, et:et + 1]).then_inc(m_act.sem, 1)

            def conv_tanh(k, j):
                act.wait_ge(m_dve.sem, m_dve.at(k, f"c2b{j}"))
                if j >= 2:
                    act.wait_ge(m_dve.sem, m_dve.at(k, f"silu{j - 2}"))
                act.activation(th[:, j % 2, :], xc2[:, 2 * j:2 * j + 2, :].rearrange("p c w -> p (c w)"),
                               ACT.Tanh, scale=0.5).then_inc(m_act.sem, 1)

            def x_rows(k):
                act.wait_ge(m_pe.sem, m_pe.at(k, "xp"))
                if due(count := h_pe.at(k - 1, "dt1_1")):
                    act.wait_ge(h_pe.sem, count)
                if due(count := 16 * k):
                    act.wait_ge(b_stored, count)
                act.activation(xdbl[0:XR, :], bank("xp")[0:XR, 0:W], ACT.Copy,
                               scale=xscale[:, 0:1]).then_inc(m_act.sem, 1)

            def c_rows(k):
                act.wait_ge(h_pe.sem, h_pe.at(k, "C"))
                if due(count := h_dve.at(k - 1, "C")):
                    act.wait_ge(h_dve.sem, count)
                act.activation(c_next[:, :, :],
                               bank("C").rearrange("p (q c) -> p q c", c=P)[:, 0:TB, R + NS:XR],
                               ACT.Copy).then_inc(h_act.sem, 1)

            def softplus(k, hf):
                if due(count := NEXP * (k - 1) + NEXP // 2 * (hf + 1)):
                    act.wait_ge(decay_done, count)
                if due(count := 2 * NSTEP * (k - 1) + NSTEP * (hf + 1)):
                    act.wait_ge(dbx_done, count)
                for e in range(HT):
                    if e % 2 == 0:
                        act.wait_ge(h_pe.sem, h_pe.at(k, f"dt{hf}_{e // 2}"))
                    act.activation(delta[:, hf, e, :],
                                   bank(f"dt{hf}_{e // 2}")[:, (e % 2) * W:(e % 2 + 1) * W], ACT.Identity,
                                   bias=evec[:, 1, HT * hf + e:HT * hf + e + 1]).then_inc(h_act.sem, 1)
                act.wait_ge(h_act.sem, h_act.at(k, f"xd{hf}"))
                act.activation(u[:, hf, :, :], delta[:, hf, :, :], ACT.Abs).then_inc(h_act.sem, 1)
                act.wait_ge(h_act.sem, h_act.at(k, f"abs{hf}"))
                act.activation(u[:, hf, :, :], u[:, hf, :, :], ACT.Exp, scale=-1.0).then_inc(h_act.sem, 1)
                act.wait_ge(h_act.sem, h_act.at(k, f"exp{hf}"))
                act.activation(u[:, hf, :, :], u[:, hf, :, :], ACT.Ln, bias=1.0).then_inc(h_act.sem, 1)

            def skip_columns(k, hf):
                if due(count := f_pe[1].at(k - 2, "k1")):
                    act.wait_ge(f_pe[1].sem, count)
                if due(count := h_pe.at(k - (1 - hf), f"sd{1 - hf}_1")):
                    act.wait_ge(h_pe.sem, count)
                for e in range(HT):
                    et = HT * hf + e
                    act.activation(ffn_mix[1][:, e, :], xc2[:, et, :], ACT.Copy,
                                   scale=evec[:, 3, et:et + 1]).then_inc(h_act.sem, 1)

            def skip_rows(k, hf, tb):
                act.wait_ge(h_pe.sem, h_pe.at(k, f"sd{hf}_{tb}"))
                if due(count := y_pe.at(k - 1, f"T{2 * hf + 1}")):
                    act.wait_ge(y_pe.sem, count)
                act.activation(y_rows[:, hf, tb, :], bank(f"sd{hf}_{tb}"), ACT.Copy).then_inc(h_act.sem, 1)

            def gate_tanh(k, j):
                act.wait_ge(z_pe.sem, z_pe.at(k, f"{j}"))
                if j >= 2:
                    act.wait_ge(z_dve.sem, z_dve.at(k, f"{j - 2}"))
                else:
                    if due(count := z_dve.at(k - 1, f"{j + 2}")):
                        act.wait_ge(z_dve.sem, count)
                act.activation(zth[:, j % 2, :], bank(f"z{j}"), ACT.Tanh, scale=0.5).then_inc(z_act.sem, 1)

            def decays(it, s, lo, hi):
                hf, n = divmod(s, NS)
                act.wait_ge(h_dve.sem, h_dve.at(it, f"delta{hf}"))
                for e in range(lo, hi):
                    q = HT * s + e
                    before = q - DAB if q >= DAB else {0: -2, 1: -1, 2: -3}[q]
                    if due(count := NEXP * it + before + 1):
                        act.wait_ge(scan_done, count)
                    o = decay[:, q % DAB, 0:B * SEG].rearrange("p (b s) -> p b s", b=B)
                    act.activation(o[:, :, 1:SEG], col3(delta[:, hf, e, :]), ACT.Exp,
                                   scale=neg_a[:, HT * hf + e, n:n + 1]).then_inc(decay_done, 1)

            def save(it, s, pair):
                if due(count := NEXP * it + HT * (s + 1)):
                    act.wait_ge(scan_done, count)
                if due(count := 2 * NSTEP * it + 2 * s + 1):
                    act.wait_ge(dbx_done, count)
                act.activation(state[:, pair, s, :, :], h[:, s % 2, :, :, T], ACT.Copy).then_inc(saved, 1)

            def body(it, pair):
                scan, front, back = has(it, 0), has(it, 1), has(it, -1)
                f, b = it + 1, it - 1
                for s in range(NSTEP):
                    if scan:
                        decays(it, s, 0, HT)
                        if s >= 1:
                            save(it, s - 1, pair)
                    if scan:
                        if s == 1:
                            softplus(it, 1)
                        if s == 2:
                            skip_columns(it, 1)
                        if s == 4:
                            skip_rows(it, 1, 0)
                            skip_rows(it, 1, 1)
                        if s in (11, 12):
                            gate_tanh(it, s - 11)
                        if s in (17, 18):
                            gate_tanh(it, s - 15)
                    if front:
                        if s == 2:
                            ffn_columns(0, f, (pair + 1) % PAIRS)
                        if s == 3:
                            ffn_before(0, f, 0)
                        if s in (7, 8):
                            ffn_tanh(0, f, s - 7)
                        if s == 8:
                            ffn_before(0, f, 1)
                    if front:
                        if s in (9, 10):
                            ffn_relu2(0, f, s - 9)
                    if back:
                        if s == 10:
                            ffn_columns(1, b, (pair - 1) % PAIRS)
                        if s == 11:
                            ffn_before(1, b, 0, scan)
                        if s in (15, 16):
                            ffn_tanh(1, b, s - 15)
                        if s == 16:
                            ffn_before(1, b, 1)
                    if front:
                        if s == 19:
                            mamba_columns(f)
                        if 21 <= s < 25:
                            conv_tanh(f, s - 21)
                        if 20 <= s < 24:
                            conv_start(f, s - 20, (pair + 1) % PAIRS)
                    if back and s in (24, 25):
                        ffn_relu2(1, b, s - 24)
                    if front:
                        if s == 28:
                            x_rows(f)
                        if s == 29:
                            c_rows(f)
                        if s == 30:
                            softplus(f, 0)
                            skip_columns(f, 0)
                    if s == 31:
                        if scan:
                            save(it, s, pair)
                        if front:
                            skip_rows(f, 0, 0)
                            skip_rows(f, 0, 1)

            run(body, act)

        @block.vector
        def _(dve):
            for q in range(DAB):
                dve.memset(decay[:, q, 0:B * SEG], 0.0).then_inc(init_dve, 1)
            dve.wait_ge(v_loaded, 16 * 9)
            dve.tensor_scalar(vec[:, 2:4, :], vec[:, 0:2, :], -1.0, 1.0, ALU.mult,
                              ALU.add).then_inc(init_dve, 1)
            dve.tensor_scalar(evec[:, 3, :], evec[:, 2, :], 0.5, None, ALU.mult).then_inc(init_dve, 1)
            dve.wait_ge(init_dve, 5)

            def norm_stats(q, marks, k, src):
                for tb in range(TB):
                    dve.bn_stats(stats[q][:, tb, :], src[:, tb, :]).then_inc(marks.sem, 1)
                for tb in range(TB):
                    dve.wait_ge(marks.sem, marks.at(k, f"st{tb}"))
                    dve.sem_inc(passed_dve, 1)
                    dve.bn_aggr(mv[q][:, tb, :], stats[q][:, tb, :]).then_inc(marks.sem, 1)

            def normalise(q, pool_marks, marks, k, src, dst, r0):
                dve.wait_ge(pool_marks.sem, pool_marks.at(k, f"y{NEWTON - 1}"))
                for tb in range(TB):
                    dve.tensor_scalar(dst[:, tb, :], src[:, tb, :], mv[q][:, tb, 0:1],
                                      rs[q][:, r0 + tb:r0 + tb + 1], ALU.subtract,
                                      ALU.mult).then_inc(marks.sem, 1)

            def ffn_stats(i, k, src):
                if due(count := f_pool[i].at(k - 1, "v")):
                    dve.wait_ge(f_pool[i].sem, count)
                norm_stats(i, f_dve[i], k, src)

            def ffn_norm(i, k, src):
                if i == 0:
                    if due(count := m_pe.at(k - 1, "T1")):
                        dve.wait_ge(m_pe.sem, count)
                else:
                    if due(count := f_dve[i].at(k - 1, "o1")):
                        dve.wait_ge(f_dve[i].sem, count)
                normalise(i, f_pool[i], f_dve[i], k, src, ffn_row[i], 0)

            def ffn_mix_in(i, k, q):
                for ct in range(CT):
                    dve.wait_ge(f_act[i].sem, f_act[i].at(k, f"{'pr' if q == 0 else 'pk'}{ct}"))
                    m = col3(ffn_mix[i][:, ct, :])
                    dve.scalar_tensor_tensor(out=m, in0=fcol(i, ct, 1), scalar=vec[:, q, ct:ct + 1],
                                             in1=m, op0=ALU.mult, op1=ALU.add).then_inc(f_dve[i].sem, 1)

            def ffn_gate(i, k, tb):
                dve.wait_ge(f_pe[i].sem, f_pe[i].at(k, f"v{tb}"))
                dve.wait_ge(f_act[i].sem, f_act[i].at(k, f"th{tb}"))
                g = ffn_row[i][:, tb, :]
                dve.scalar_tensor_tensor(out=g, in0=g, scalar=1.0, in1=bank(f"f{i}v{tb}"), op0=ALU.add,
                                         op1=ALU.mult).then_inc(f_dve[i].sem, 1)

            def ffn_add(i, k, tb, xx):
                dve.wait_ge(f_dve[i].sem, f_dve[i].at(k, f"g{tb}"))
                dve.scalar_tensor_tensor(out=xx[:, tb, :], in0=ffn_row[i][:, tb, :], scalar=0.25,
                                         in1=xx[:, tb, :], op0=ALU.mult,
                                         op1=ALU.add).then_inc(f_dve[i].sem, 1)

            def mamba_norm(k):
                if due(count := k):
                    dve.wait_ge(res_kept, count)
                if due(count := m_pool.at(k - 1, "res")):
                    dve.wait_ge(m_pool.sem, count)
                normalise(2, m_pool, m_dve, k, xin, res, 0)
                normalise(2, m_pool, m_dve, k, xin, ffn_row[0], TB)

            def conv_taps(k, j):
                for q in range(KC - 1):
                    for c in range(2):
                        et = 2 * j + c
                        if q == 0:
                            dve.wait_ge(m_act.sem, m_act.at(k, f"tap{'ab'[c]}{j}"))
                        else:
                            dve.wait_ge(m_dve.sem, m_dve.at(k, f"c{q - 1}{'ab'[c]}{j}"))
                        o = col3(xc2[:, et, :])
                        dve.scalar_tensor_tensor(out=o, in0=xs_pad[:, j % 2, c, :, q:q + T],
                                                 scalar=conv_sb[:, et, q:q + 1], in1=o, op0=ALU.mult,
                                                 op1=ALU.add).then_inc(m_dve.sem, 1)

            def conv_silu(k, j):
                dve.wait_ge(m_act.sem, m_act.at(k, f"th{j}"))
                o = xc2[:, 2 * j:2 * j + 2, :].rearrange("p c w -> p (c w)")
                dve.scalar_tensor_tensor(out=o, in0=th[:, j % 2, :], scalar=1.0, in1=o, op0=ALU.add,
                                         op1=ALU.mult).then_inc(m_dve.sem, 1)

            def softplus_sum(k, hf):
                dve.wait_ge(h_act.sem, h_act.at(k, f"ln{hf}"))
                d = delta[:, hf, :, :].rearrange("p e w -> p (e w)")
                dve.scalar_tensor_tensor(out=d, in0=d, scalar=0.0,
                                         in1=u[:, hf, :, :].rearrange("p e w -> p (e w)"), op0=ALU.max,
                                         op1=ALU.add).then_inc(h_dve.sem, 1)

            def gate_silu(k, j):
                dve.wait_ge(z_act.sem, z_act.at(k, f"{j}"))
                if due(count := y_pe.at(k - 1, "o1")):
                    dve.wait_ge(y_pe.sem, count)
                dve.scalar_tensor_tensor(out=gate[:, 2 * j:2 * j + 2, :].rearrange("p c w -> p (c w)"),
                                         in0=zth[:, j % 2, :], scalar=1.0, in1=bank(f"z{j}"), op0=ALU.add,
                                         op1=ALU.mult).then_inc(z_dve.sem, 1)

            def gate_y(k, j):
                dve.wait_ge(y_pe.sem, y_pe.at(k, f"T{j}"))
                dve.wait_ge(z_dve.sem, z_dve.at(k, f"{j}"))
                g = gate[:, 2 * j:2 * j + 2, :].rearrange("p c w -> p (c w)")
                dve.tensor_tensor(g, g, bank(f"YT{j}"), ALU.mult).then_inc(y_dve.sem, 1)

            def out_add(k, tb):
                dve.wait_ge(y_pe.sem, y_pe.at(k, f"o{tb}"))
                if due(count := k + 1):
                    dve.wait_ge(res_kept, count)
                if due(count := 16 * TB * k):
                    dve.wait_ge(out_stored, count)
                dve.scalar_tensor_tensor(out=xout[:, tb, :], in0=bank(f"o{tb}"), scalar=0.5,
                                         in1=res_prev[:, tb, :], op0=ALU.mult,
                                         op1=ALU.add).then_inc(y_dve.sem, 1)

            def scan(it, s, lo, hi):
                for e in range(lo, hi):
                    q = HT * s + e
                    if e == 0:
                        if due(count := 2 * NSTEP * it + 2 * s + 2):
                            dve.wait_ge(dbx_done, count)
                        if due(count := NSTT * it + TB * (s - 1)):
                            dve.wait_ge(h_turned, count)
                        if due(count := NSTEP * it + s - 1):
                            dve.wait_ge(saved, count)
                    if due(count := NEXP * it + q + 1):
                        dve.wait_ge(decay_done, count)
                    dve.tensor_tensor_scan(h[:, s % 2, e, :, :].rearrange("p b s -> p (b s)"),
                                           decay[:, q % DAB, 0:B * SEG],
                                           dbx[:, s % 2, e, :, :].rearrange("p b s -> p (b s)"), 0.0,
                                           ALU.mult, ALU.add).then_inc(scan_done, 1)

            def add_y(it, s, tb):
                hf, n = divmod(s, NS)
                if due(count := NSTT * it + TB * s + tb + 1):
                    dve.wait_ge(h_turned, count)
                if n == 0:
                    dve.wait_ge(h_act.sem, h_act.at(it, f"yb{hf}"))
                    dve.wait_ge(h_dve.sem, h_dve.at(it, "C"))
                else:
                    if due(count := NSTT * it + TB * (s - 1) + tb + 1):
                        dve.wait_ge(y_added, count)
                yy = y_rows[:, hf, tb, :]
                dve.scalar_tensor_tensor(out=yy, in0=h_rows[:, tb, :], scalar=c_now[:, tb, n:n + 1],
                                         in1=yy, op0=ALU.mult, op1=ALU.add).then_inc(y_added, 1)

            def body(it, pair):
                scn, front, back = has(it, 0), has(it, 1), has(it, -1)
                f, b = it + 1, it - 1
                for s in range(NSTEP):
                    for part in range(2):
                        if scn:
                            scan(it, s, 2 * part, 2 * part + 2)
                        if s == 0 and back:
                            add_y(b, NSTEP - 1, part)
                        elif s > 0 and scn:
                            add_y(it, s - 1, part)
                    if s == 0 and scn:
                        dve.wait_ge(h_act.sem, h_act.at(it, "C"))
                        if due(count := NSTT * it):
                            dve.wait_ge(y_added, count)
                        dve.tensor_copy(c_now[:, :, :], c_next[:, :, :]).then_inc(h_dve.sem, 1)
                    if front and s == 0:
                        dve.wait_ge(x_loaded, (it + 2) * (16 * TB))
                        ffn_stats(0, f, xin)
                        ffn_norm(0, f, xin)
                    if back and s == 2:
                        gate_y(b, 2)
                        gate_y(b, 3)
                    if scn and s == 2:
                        softplus_sum(it, 1)
                    if front and s == 4:
                        ffn_mix_in(0, f, 0)
                    if back:
                        if s == 4:
                            out_add(b, 0)
                        if s == 6:
                            out_add(b, 1)
                            dve.wait_ge(y_dve.sem, y_dve.at(b, "x1"))
                            ffn_stats(1, b, xout)
                        if s == 8:
                            ffn_norm(1, b, xout)
                    if front and s == 8:
                        ffn_mix_in(0, f, 1)
                    if scn:
                        if s in (11, 12):
                            gate_silu(it, s - 11)
                        if s in (17, 18):
                            gate_silu(it, s - 15)
                    if back and s == 12:
                        ffn_mix_in(1, b, 0)
                    if front:
                        if s in (13, 14):
                            ffn_gate(0, f, s - 13)
                        if s == 14:
                            ffn_add(0, f, 0, xin)
                            ffn_add(0, f, 1, xin)
                            dve.wait_ge(f_dve[0].sem, f_dve[0].at(f, "o1"))
                            if due(count := m_pool.at(f - 1, "v2")):
                                dve.wait_ge(m_pool.sem, count)
                            norm_stats(2, m_dve, f, xin)
                        if s == 16:
                            mamba_norm(f)
                    if back and s == 17:
                        ffn_mix_in(1, b, 1)
                    if scn and s == 18:
                        gate_y(it, 0)
                        gate_y(it, 1)
                    if front:
                        if 21 <= s < 25:
                            conv_silu(f, s - 21)
                        if 20 <= s < 24:
                            conv_taps(f, s - 20)
                    if back:
                        if s in (26, 27):
                            ffn_gate(1, b, s - 26)
                        if s == 27:
                            ffn_add(1, b, 0, xout)
                            ffn_add(1, b, 1, xout)
                    if front and s == 31:
                        softplus_sum(f, 0)

            run(body, dve)

        @block.gpsimd
        def _(pool):
            pool.memset(ident[:, :], 0.0).then_inc(init_pool, 1)
            pool.memset(wdt_sb[:, :], 0.0).then_inc(init_pool, 1)
            pool.wait_ge(init_pool, 1)
            pool.affine_select(out=ident[:, :], in_=ident[:, :], compare_op=ALU.not_equal, fill=1.0,
                               base=0, pattern=[[-1, P]], channel_multiplier=1).then_inc(init_pool, 1)
            pool.memset(xdbl[:, :], 0.0).then_inc(init_pool, 1)
            pool.memset(state[:, :, :, :, :], 0.0).then_inc(init_pool, 1)
            pool.memset(xs_last[:, :, :, :, :], 0.0).then_inc(init_pool, 1)
            for i in range(2):
                pool.memset(ffn_last[i][:, :, :, :], 0.0).then_inc(init_pool, 1)
            pool.memset(xscale[:, :], 0.5).then_inc(init_pool, 1)
            pool.wait_ge(init_pool, 9)
            pool.affine_select(out=xscale[:, :], in_=xscale[:, :], compare_op=ALU.is_gt, fill=0.25,
                               base=R, pattern=[[0, 1]], channel_multiplier=-1).then_inc(init_pool, 1)
            pool.wait_ge(init_pool, 10)
            pool.affine_select(out=xscale[:, :], in_=xscale[:, :], compare_op=ALU.is_gt, fill=0.5,
                               base=R + NS, pattern=[[0, 1]], channel_multiplier=-1).then_inc(init_pool, 1)
            pool.wait_ge(init_pool, 11)

            def rsqrt(q, marks, k, n):
                v, t, y = nv[q][:, 0:n], nt[q][:, 0:n], rs[q][:, 0:n]
                pool.wait_ge(marks.sem, marks.at(k, marks.names[marks.names.index("guess") - 1]))
                pool.sem_inc(passed_pool, 1)
                pool.tensor_scalar(y.bitcast(I32), v.bitcast(I32), -0.5, RSQRT_GUESS, ALU.mult,
                                   ALU.add).then_inc(marks.sem, 1)
                before = "guess"
                for i in range(NEWTON):
                    pool.wait_ge(marks.sem, marks.at(k, before))
                    pool.tensor_tensor(t, y, y, ALU.mult).then_inc(marks.sem, 1)
                    pool.wait_ge(marks.sem, marks.at(k, f"yy{i}"))
                    pool.tensor_tensor(t, t, v, ALU.mult).then_inc(marks.sem, 1)
                    pool.wait_ge(marks.sem, marks.at(k, f"vyy{i}"))
                    pool.sem_inc(passed_pool, 1)
                    pool.tensor_scalar(t, t, -0.5, 1.5, ALU.mult, ALU.add).then_inc(marks.sem, 1)
                    pool.wait_ge(marks.sem, marks.at(k, f"half{i}"))
                    pool.tensor_tensor(y, y, t, ALU.mult).then_inc(marks.sem, 1)
                    before = f"y{i}"

            def ffn_rstd(i, k):
                if due(count := f_dve[i].at(k - 1, "ln1")):
                    pool.wait_ge(f_dve[i].sem, count)
                pool.wait_ge(f_dve[i].sem, f_dve[i].at(k, "mv1"))
                pool.sem_inc(passed_pool, 1)
                pool.tensor_scalar(nv[i][:, 0:TB], mv[i][:, :, 1], 1.0, EPS, ALU.mult,
                                   ALU.add).then_inc(f_pool[i].sem, 1)
                rsqrt(i, f_pool[i], k, TB)

            def mamba_rstd(k):
                if due(count := m_dve.at(k - 1, "in1")):
                    pool.wait_ge(m_dve.sem, count)
                pool.wait_ge(m_dve.sem, m_dve.at(k, "mv1"))
                pool.sem_inc(passed_pool, 1)
                pool.tensor_scalar(nv[2][:, 0:TB], mv[2][:, :, 1], 1.0, EPS, ALU.mult,
                                   ALU.add).then_inc(m_pool.sem, 1)
                pool.tensor_scalar(nv[2][:, TB:2 * TB], mv[2][:, :, 1], 1.0 + EPS, EPS * EPS, ALU.mult,
                                   ALU.add).then_inc(m_pool.sem, 1)
                rsqrt(2, m_pool, k, 2 * TB)

            def make_res(k):
                pool.wait_ge(m_dve.sem, m_dve.at(k, "ln1"))
                pool.tensor_tensor(res[:, :, :], res[:, :, :], xin[:, :, :], ALU.add).then_inc(m_pool.sem, 1)

            def keep_res(k):
                pool.wait_ge(m_pool.sem, m_pool.at(k, "res"))
                if due(count := y_dve.at(k - 1, "x1")):
                    pool.wait_ge(y_dve.sem, count)
                    pool.sem_inc(passed_pool, 1)
                pool.tensor_copy(res_prev[:, :, :], res[:, :, :]).then_inc(res_kept, 1)

            def make_u(k, hf):
                pool.wait_ge(h_dve.sem, h_dve.at(k, f"delta{hf}"))
                pool.wait_ge(m_dve.sem, m_dve.at(k, "silu3"))
                pool.tensor_tensor(u[:, hf, :, :], delta[:, hf, :, :], xc2[:, HT * hf:HT * (hf + 1), :],
                                   ALU.mult).then_inc(h_pool.sem, 1)

            def products(it, s, pair):
                hf, n = divmod(s, NS)
                if due(count := NEXP * it + HT * (s - 1)):
                    pool.wait_ge(scan_done, count)
                if due(count := NSTEP * (it - PAIRS) + s + 1):
                    pool.wait_ge(saved, count)
                    pool.sem_inc(passed_pool, 1)
                pool.tensor_copy(dbx[:, s % 2, :, :, 0], state[:, pair, s, :, :]).then_inc(dbx_done, 1)
                j = s // NBG
                if s % NBG == 0:
                    pool.wait_ge(b_loaded[j % 2], it * (16 * 4) + 16 * (j // 2 + 1))
                if n == 0:
                    pool.wait_ge(h_pool.sem, h_pool.at(it, f"u{hf}"))
                bb = b_all[:, j % 2, s % NBG, :].rearrange("p (b t) -> p b t", b=B)
                pool.tensor_tensor(dbx[:, s % 2, :, :, 1:SEG],
                                   u[:, hf, :, :].rearrange("p e (b t) -> p e b t", b=B),
                                   bb.unsqueeze(1).broadcast_to([P, HT, B, T]),
                                   ALU.mult).then_inc(dbx_done, 1)

            def body(it, pair):
                scn, front, back = has(it, 0), has(it, 1), has(it, -1)
                f, b = it + 1, it - 1
                for s in range(NSTEP):
                    if scn:
                        products(it, s, pair)
                    if front and s == 0:
                        ffn_rstd(0, f)
                    if scn:
                        if s == 3:
                            make_u(it, 1)
                        if s == 8:
                            keep_res(it)
                    if back and s == 6:
                        ffn_rstd(1, b)
                    if front:
                        if s == 14:
                            mamba_rstd(f)
                        if s == 17:
                            make_res(f)
                        if s == 31:
                            make_u(f, 0)

            run(body, pool)


def kernel(L0_attn_x, L0_attn_ln_w, L0_attn_ln_b, L0_attn_W_in, L0_attn_W_conv, L0_attn_b_conv,
           L0_attn_W_xproj, L0_attn_W_dt, L0_attn_b_dt, L0_attn_A_log, L0_attn_D_skip, L0_attn_W_out,
           L0_ffn_W_r, L0_ffn_W_k, L0_ffn_W_v, L0_ffn_mu_r, L0_ffn_mu_k):
    import numpy as np
    import concourse.bacc as bacc
    from concourse.bass_utils import run_bass_kernel_spmd

    def by_tile(v):
        return np.asarray(v).reshape(-1, P).T

    arrays = {
        "x": L0_attn_x, "mu_r": by_tile(L0_ffn_mu_r), "mu_k": by_tile(L0_ffn_mu_k),
        "w_r": np.asarray(L0_ffn_W_r).T, "w_k": np.asarray(L0_ffn_W_k).T,
        "w_v": np.asarray(L0_ffn_W_v).T, "ln_w": by_tile(L0_attn_ln_w), "ln_b": by_tile(L0_attn_ln_b),
        "w_in": np.asarray(L0_attn_W_in).T, "w_conv": L0_attn_W_conv, "b_conv": by_tile(L0_attn_b_conv),
        "w_x": np.asarray(L0_attn_W_xproj).T, "w_dt": np.asarray(L0_attn_W_dt).T,
        "b_dt": by_tile(L0_attn_b_dt), "a_log": L0_attn_A_log, "d_skip": by_tile(L0_attn_D_skip),
        "w_out": np.asarray(L0_attn_W_out).T,
    }
    arrays = {f"in_{n}": np.ascontiguousarray(a) for n, a in arrays.items()}
    nc = bacc.Bacc("TRN2", target_bir_lowering=False, num_devices=1)
    args = [nc.dram_tensor(n, a.shape, mybir.dt.from_np(a.dtype), kind="ExternalInput").ap()
            for n, a in arrays.items()]
    out = nc.dram_tensor("out_0", tuple(L0_attn_x.shape), F32, kind="ExternalOutput").ap()
    build(nc, *args, out)
    r = run_bass_kernel_spmd(nc, [arrays], core_ids=[0])
    return r.results[0]["out_0"]
```

```python
from contextlib import ExitStack

import concourse.bass as bass
from concourse import mybir

ALU = mybir.AluOpType
ACT = mybir.ActivationFunctionType
F32 = mybir.dt.float32
I32 = mybir.dt.int32

P = 128
T = 128
SEG = T + 1
EPS = 1e-5
RSQRT_GUESS = 1597463007.0
NEWTON = 4


class Marks:

    def __init__(self, sem, names):
        self.sem, self.names = sem, names.split() if isinstance(names, str) else names
        assert len(set(self.names)) == len(self.names)

    def at(self, chunk, name):
        return chunk * len(self.names) + (self.names.index(name) + 1)


def due(value):
    return not isinstance(value, int) or value > 0


def build(nc, x, mu_r, mu_k, w_r, w_k, w_v, ln_w, ln_b, w_in, w_conv, b_conv, w_x, w_dt, b_dt,
          a_log, d_skip, w_out, out):
    BATCHES, L, D = x.shape
    E, NS = a_log.shape
    R = w_dt.shape[0]
    KC = w_conv.shape[1]
    B = 2
    PAIRS = BATCHES // B
    NCH = L // T * PAIRS
    W = B * T
    CT, ET = D // P, E // P
    HT = ET // 2
    TB = W // P
    NSTEP = 2 * NS
    XR = R + 2 * NS
    NEXP, NSTT = NSTEP * HT, NSTEP * TB
    RING = 4
    LAG = 2
    SAVE = 3
    BANKS = 4
    NBG = 2
    NG = NSTEP // NBG
    assert TB == 2 and CT == 4 and HT == 4 and T == P and PAIRS == 2 and R == 32 and NS == 16 and XR == 64

    with ExitStack() as ctx:
        def sb(name, shape, dt=F32):
            return ctx.enter_context(nc.sbuf_tensor(name, shape, dt))

        def ps(name, shape):
            return ctx.enter_context(nc.psum_tensor(name, shape, F32))

        def sem(name):
            return ctx.enter_context(nc.semaphore(name))

        h_rows = ps("h_rows", [P, 2, TB, 512])
        mm = ps("mm", [P, BANKS, 512])

        wr_sb, wk_sb, wv_sb = (sb(n, [P, CT, D]) for n in ("wr_sb", "wk_sb", "wv_sb"))
        win_sb = sb("win_sb", [P, CT, 2 * E])
        wx_sb = sb("wx_sb", [P, ET, XR])
        wdt_sb = sb("wdt_sb", [P, E])
        wout_sb = sb("wout_sb", [P, ET, D])
        ident = sb("ident", [P, P])
        vec = sb("vec", [P, 6, CT])
        conv_sb = sb("conv_sb", [P, ET, KC])
        evec = sb("evec", [P, 4, ET])
        neg_a = sb("neg_a", [P, ET, NS])
        xscale = sb("xscale", [XR, 1])

        xin = sb("xin", [P, TB, D])
        res = sb("res", [P, PAIRS, TB, D])
        xout = sb("xout", [P, TB, D])
        ffn_row = [sb(f"ffn_row{i}", [P, TB, D]) for i in range(2)]
        ffn_col = [sb(f"ffn_col{i}", [P, CT, B * SEG]) for i in range(2)]
        ffn_mix = [sb(f"ffn_mix{i}", [P, CT, W]) for i in range(2)]
        ffn_last = [sb(f"ffn_last{i}", [P, PAIRS, CT, B]) for i in range(2)]
        stats = [sb(f"stats{i}", [P, TB, 6]) for i in range(3)]
        mv = [sb(f"mv{i}", [P, TB, 2]) for i in range(3)]
        nv = [sb(f"nv{i}", [P, 2 * TB]) for i in range(3)]
        nt = [sb(f"nt{i}", [P, 2 * TB]) for i in range(3)]
        rs = [sb(f"rs{i}", [P, 2 * TB]) for i in range(3)]
        xn_col = sb("xn_col", [P, CT, W])
        xs_pad = sb("xs_pad", [P, 2, 2, B, T + KC - 1])
        xs_last = sb("xs_last", [P, PAIRS, ET, B, KC - 1])
        xc2 = sb("xc2", [P, ET, W])
        th = sb("th", [P, 2, 512])
        zth = sb("zth", [P, 512])
        gate = sb("gate", [P, ET, W])
        xdbl = sb("xdbl", [P, W])
        c_rows = sb("c_rows", [P, PAIRS, TB, NS])
        delta = sb("delta", [P, 2, HT, W])
        u = sb("u", [P, 2, HT, W])
        b_all = sb("b_all", [P, 2, NBG, W])
        decay = sb("decay", [P, 2, HT, B, SEG])
        h = sb("h", [P, RING, HT, B, SEG])
        state = sb("state", [P, PAIRS, NSTEP, HT, B])
        y_rows = sb("y_rows", [P, 2, TB, 512])

        b_dram = nc.dram_tensor("b_scratch", (NCH, NS * W), F32).ap()

        w_loaded, v_loaded = sem("w_loaded"), sem("v_loaded")
        x_loaded, out_stored = sem("x_loaded"), sem("out_stored")
        b_stored = sem("b_stored")
        b_loaded = [sem("b_loaded0"), sem("b_loaded1")]
        init_pool, init_dve, init_act = sem("init_pool"), sem("init_dve"), sem("init_act")

        passed_sp, passed_dve, passed_pool = sem("passed_sp"), sem("passed_dve"), sem("passed_pool")

        decay_done = sem("decay_done")
        dbx_done = sem("dbx_done")
        scan_done = sem("scan_done")
        saved = sem("saved")
        h_turned = sem("h_turned")
        y_added = sem("y_added")

        newton = ["guess"] + [f"{q}{i}" for i in range(NEWTON) for q in ("yy", "vyy", "half", "y")]
        f_pe = [Marks(sem(f"ffn{i}_pe"), "T0 T1 k0 k1 r0 r1 v0 v1") for i in range(2)]
        f_act = [Marks(sem(f"ffn{i}_act"), "xn0 xn1 lead last pk0 pk1 pk2 pk3 "
                       "pr0 pr1 pr2 pr3 rel0 sq0 rel1 sq1 th0 th1") for i in range(2)]
        f_dve = [Marks(sem(f"ffn{i}_dve"), "st0 st1 mv0 mv1 ln0 ln1 xk0 xk1 xk2 xk3 "
                       "xr0 xr1 xr2 xr3 g0 g1 o0 o1") for i in range(2)]
        f_pool = [Marks(sem(f"ffn{i}_pool"), ["v"] + newton) for i in range(2)]
        m_pe = Marks(sem("mamba_pe"), "T0 T1 xs0 xs1 xs2 xs3 xp")
        m_act = Marks(sem("mamba_act"), "xn0 xn1 xn2 xn3 raw0 lead0 last0 tapa0 tapb0 "
                      "raw1 lead1 last1 tapa1 tapb1 th0 raw2 lead2 last2 tapa2 tapb2 th1 "
                      "raw3 lead3 last3 tapa3 tapb3 th2 th3 xp")
        taps = [f"c{q}{c}" for q in range(KC - 1) for c in "ab"]
        m_dve = Marks(sem("mamba_dve"), ["st0", "st1", "mv0", "mv1", "ln0", "ln1", "in0", "in1"] + [
            t for do in "t0 t1 s0 s1 t2 t3 s2 s3".split()
            for t in ([q + do[1] for q in taps] if do[0] == "t" else ["silu" + do[1]])])
        m_pool = Marks(sem("mamba_pool"), ["v", "v2"] + newton + ["res"])
        h_pe = Marks(sem("half_pe"), "C dt0_0 dt0_1 sd0_0 sd0_1 dt1_0 dt1_1 sd1_0 sd1_1")
        h_act = Marks(sem("half_act"), ["C"] + [
            f"{q}{hf}" for hf in range(2)
            for q in ("xa", "xb", "xc", "xd", "abs", "exp", "ln", "da", "db", "dc", "dd", "ya", "yb")])
        h_dve = Marks(sem("half_dve"), "delta0 delta1")
        h_pool = Marks(sem("half_pool"), "u0 u1")
        z_pe = Marks(sem("gate_pe"), "0 1 2 3")
        z_act = Marks(sem("gate_act"), "0 1 2 3")
        z_dve = Marks(sem("gate_dve"), "0 1 2 3")
        y_pe = Marks(sem("y_pe"), "T0 T1 T2 T3 o0 o1")
        y_dve = Marks(sem("y_dve"), "g0 g1 g2 g3 x0 x1")

        GROUPS = [("f0T0", 1, f_act[0], "xn0"), ("f0T1", 1, f_act[0], "xn1"),
                  ("z0", 0, z_dve, "0"), ("z1", 0, z_dve, "1"),
                  ("YT2", -1, y_dve, "g2"), ("YT3", -1, y_dve, "g3"),
                  ("f0k0", 1, f_act[0], "rel0"), ("f0k1", 1, f_act[0], "rel1"),
                  ("f0r0", 1, f_act[0], "th0"), ("f0r1", 1, f_act[0], "th1"),
                  ("dt1_0", 0, h_act, "xb1"), ("f0v0", 1, f_dve[0], "g0"),
                  ("dt1_1", 0, h_act, "xd1"), ("f0v1", 1, f_dve[0], "g1"),
                  ("o0", -1, y_dve, "x0"), ("o1", -1, y_dve, "x1"),
                  ("z2", 0, z_dve, "2"), ("z3", 0, z_dve, "3"),
                  ("mT0", 1, m_act, "xn1"), ("mT1", 1, m_act, "xn3"),
                  ("sd1_0", 0, h_act, "ya1"), ("sd1_1", 0, h_act, "yb1"),
                  ("xs0", 1, m_act, "tapb0"), ("xs1", 1, m_act, "tapb1"),
                  ("f1T0", -1, f_act[1], "xn0"), ("f1T1", -1, f_act[1], "xn1"),
                  ("xs2", 1, m_act, "tapb2"), ("xs3", 1, m_act, "tapb3"),
                  ("f1k0", -1, f_act[1], "rel0"), ("f1k1", -1, f_act[1], "rel1"),
                  ("xp", 1, m_act, "xp"), ("f1r0", -1, f_act[1], "th0"), ("C", 1, h_act, "C"),
                  ("dt0_0", 1, h_act, "xb0"), ("dt0_1", 1, h_act, "xd0"),
                  ("f1r1", -1, f_act[1], "th1"),
                  ("f1v0", -1, f_dve[1], "g0"), ("f1v1", -1, f_dve[1], "g1"),
                  ("YT0", 0, y_dve, "g0"), ("YT1", 0, y_dve, "g1"),
                  ("sd0_0", 1, h_act, "ya0"), ("sd0_1", 1, h_act, "yb0")]
        SLOTS = -(-len(GROUPS) // BANKS) * BANKS
        NUMBER = {g[0]: n for n, g in enumerate(GROUPS)}

        def bank(group):
            return mm[:, NUMBER[group] % BANKS, :]

        def bank_free(it, group):
            n = NUMBER[group] - BANKS
            while True:
                if n < 0:
                    n, it = n + SLOTS, it - 1
                if n < len(GROUPS):
                    _, off, marks, name = GROUPS[n]
                    if not isinstance(it, int) or 0 <= it + off < NCH:
                        return marks.sem, marks.at(it + off, name)
                if it < -2:
                    return None
                n -= BANKS

        def soft(hf):
            return u[:, 0, :, :].rearrange("p e w -> p (e w)") if hf == 0 else \
                ffn_row[1][:, :, :].rearrange("p b d -> p (b d)")

        def mix(i, q):
            return ffn_mix[i if q == 1 else 1 - i]

        def col3(t):
            return t.rearrange("p (b t) -> p b t", b=B)

        def fcol(i, ct, lo):
            return ffn_col[i][:, ct, :].rearrange("p (b s) -> p b s", b=B)[:, :, lo:lo + T]

        def run(body, eng):
            for it in (-2, -1, 0, 1):
                body(it, it % PAIRS)
            with eng.Fori(1, NCH // PAIRS - 1) as turn:
                for pair in range(PAIRS):
                    body(turn * PAIRS + pair, pair)
            for it in (NCH - 2, NCH - 1, NCH):
                body(it, it % PAIRS)

        def has(it, off):
            return not isinstance(it, int) or 0 <= it + off < NCH

        block = ctx.enter_context(nc.Block())

        @block.sync
        def _(sp):
            def rows_of(dram, k, pair, tb):
                return dram[B * pair + tb, bass.ds((k - pair) * (T // PAIRS), T), :]

            def load_x(k, pair):
                if due(count := m_pool.at(k - 1, "res")):
                    sp.wait_ge(m_pool.sem, count)
                    sp.sem_inc(passed_sp, 1)
                if due(count := m_dve.at(k - 1, "in1")):
                    sp.wait_ge(m_dve.sem, count)
                    sp.sem_inc(passed_sp, 1)
                for tb in range(TB):
                    sp.dma_start(xin[:, tb, :], rows_of(x, k, pair, tb)).then_inc(x_loaded, 16)

            for i, v in ((0, mu_r), (1, mu_k), (4, ln_w), (5, ln_b)):
                sp.dma_start(vec[:, i, :], v).then_inc(v_loaded, 16)
            for i, v in ((0, b_conv), (1, b_dt), (2, d_skip)):
                sp.dma_start(evec[:, i, :], v).then_inc(v_loaded, 16)
            sp.dma_start(conv_sb[:, :, :], w_conv.rearrange("(t p) k -> p t k", p=P)).then_inc(v_loaded, 16)
            sp.dma_start(neg_a[:, :, :], a_log.rearrange("(t p) n -> p t n", p=P)).then_inc(v_loaded, 16)
            load_x(0, 0)
            for dst, src in ((wr_sb, w_r), (wk_sb, w_k), (wv_sb, w_v), (win_sb, w_in), (wx_sb, w_x)):
                sp.dma_start(dst[:, :, :], src.rearrange("(t p) n -> p t n", p=P)).then_inc(w_loaded, 16)
            sp.wait_ge(init_pool, 2)
            sp.dma_start(wdt_sb[0:R, :], w_dt).then_inc(w_loaded, 16)
            sp.dma_start(wout_sb[:, :, :], w_out.rearrange("(t p) n -> p t n", p=P)).then_inc(w_loaded, 16)

            def load_b(k, j):
                if j < 2:
                    if due(count := 16 * (k + 1)):
                        sp.wait_ge(b_stored, count)
                        sp.sem_inc(passed_sp, 1)
                if due(count := 2 * NSTEP * k + 2 * NBG * (j - 1)):
                    sp.wait_ge(dbx_done, count)
                    sp.sem_inc(passed_sp, 1)
                sp.dma_start(b_all[:, j % 2, :, :],
                             b_dram[bass.ds(k, 1), j % (NS // NBG) * NBG * W:(j % (NS // NBG) + 1) * NBG * W]
                             .rearrange("o (n w) -> o n w", n=NBG).broadcast_to([P, NBG, W])
                             ).then_inc(b_loaded[j % 2], 16)

            def body(it, pair):
                if has(it, 0):
                    for j in range(2, 11):
                        load_b(it, j)
                if has(it, 2) and has(it, 1):
                    load_x(it + 2, pair)
                if has(it, 0):
                    for j in range(11, NG):
                        load_b(it, j)
                if has(it, 1):
                    sp.wait_ge(m_act.sem, m_act.at(it + 1, "xp"))
                    sp.sem_inc(passed_sp, 1)
                    sp.dma_start(b_dram[bass.ds(it + 1, 1), :].rearrange("o (n w) -> (o n) w", n=NS),
                                 xdbl[R:R + NS, :]).then_inc(b_stored, 16)
                    load_b(it + 1, 0)
                    load_b(it + 1, 1)
                if has(it, -1):
                    for tb in range(TB):
                        if due(count := f_dve[1].at(it - 1, f"o{tb}")):
                            sp.wait_ge(f_dve[1].sem, count)
                            sp.sem_inc(passed_sp, 1)
                        sp.dma_start(rows_of(out, it - 1, (pair - 1) % PAIRS, tb),
                                     xout[:, tb, :]).then_inc(out_stored, 16)

            run(body, sp)
            sp.wait_ge(out_stored, 16 * TB * NCH)

        @block.tensor
        def _(pe):
            pe.wait_ge(init_pool, 3)
            pe.wait_ge(w_loaded, 16 * 7)

            def turn_rows(it, i, group, src, marks, dst_chunk, names):
                for j in range(2):
                    if free := bank_free(it, group + f"T{j}"):
                        pe.wait_ge(*free)
                    o = bank(group + f"T{j}").rearrange("p (c w) -> p c w", c=2)
                    for c in range(2):
                        for tb in range(TB):
                            ct = 2 * j + c
                            last = pe.transpose(o[:, c, tb * P:(tb + 1) * P],
                                                src[:, tb, ct * P:(ct + 1) * P], ident[:, :])
                    last.then_inc(marks.sem, 1)

            def ffn_turn(it, i, k):
                pe.wait_ge(f_dve[i].sem, f_dve[i].at(k, "ln1"))
                turn_rows(it, i, f"f{i}", ffn_row[i], f_pe[i], k, None)

            def ffn_r(it, i, k, tb):
                pe.wait_ge(f_dve[i].sem, f_dve[i].at(k, "xr3"))
                if free := bank_free(it, f"f{i}r{tb}"):
                    pe.wait_ge(*free)
                for ct in range(CT):
                    last = pe.matmul(bank(f"f{i}r{tb}"), mix(i, 0)[:, ct, tb * P:(tb + 1) * P],
                                     wr_sb[:, ct, :], start=ct == 0, stop=ct == CT - 1)
                last.then_inc(f_pe[i].sem, 1)

            def ffn_k(it, i, k, j):
                pe.wait_ge(f_dve[i].sem, f_dve[i].at(k, "xk3"))
                if free := bank_free(it, f"f{i}k{j}"):
                    pe.wait_ge(*free)
                o = bank(f"f{i}k{j}").rearrange("p (c w) -> p c w", c=2)
                for c in range(2):
                    dt = 2 * j + c
                    for ct in range(CT):
                        last = pe.matmul(o[:, c, :], wk_sb[:, ct, dt * P:(dt + 1) * P],
                                         mix(i, 1)[:, ct, :], start=ct == 0, stop=ct == CT - 1)
                last.then_inc(f_pe[i].sem, 1)

            def ffn_v(it, i, k, tb):
                pe.wait_ge(f_act[i].sem, f_act[i].at(k, "sq1"))
                if free := bank_free(it, f"f{i}v{tb}"):
                    pe.wait_ge(*free)
                for ct in range(CT):
                    last = pe.matmul(bank(f"f{i}v{tb}"), ffn_col[i][:, ct, tb * P:(tb + 1) * P],
                                     wv_sb[:, ct, :], start=ct == 0, stop=ct == CT - 1)
                last.then_inc(f_pe[i].sem, 1)

            def mamba_turn(it, k):
                pe.wait_ge(m_dve.sem, m_dve.at(k, "in1"))
                turn_rows(it, 0, "m", ffn_row[0], m_pe, k, None)

            def project(it, group, e0, marks):
                if free := bank_free(it, group):
                    pe.wait_ge(*free)
                o = bank(group).rearrange("p (c w) -> p c w", c=2)
                for c in range(2):
                    for ct in range(CT):
                        last = pe.matmul(o[:, c, :], win_sb[:, ct, e0 + c * P:e0 + (c + 1) * P],
                                         xn_col[:, ct, :], start=ct == 0, stop=ct == CT - 1)
                last.then_inc(marks.sem, 1)

            def xs(it, k, j):
                pe.wait_ge(m_act.sem, m_act.at(k, "xn3"))
                project(it, f"xs{j}", 2 * j * P, m_pe)

            def z(it, j):
                project(it, f"z{j}", E + 2 * j * P, z_pe)

            def xproj(it, k, part):
                pe.wait_ge(m_dve.sem, m_dve.at(k, f"silu{2 * part + 1}"))
                if part == 0:
                    if free := bank_free(it, "xp"):
                        pe.wait_ge(*free)
                for et in range(HT * part, HT * part + HT):
                    last = pe.matmul(bank("xp")[0:XR, 0:W], wx_sb[:, et, :], xc2[:, et, :],
                                     start=et == 0, stop=et == ET - 1)
                if part == 1:
                    last.then_inc(m_pe.sem, 1)

            def turn_c(it, k):
                pe.wait_ge(m_act.sem, m_act.at(k, "xp"))
                if free := bank_free(it, "C"):
                    pe.wait_ge(*free)
                for tb in range(TB):
                    last = pe.transpose(bank("C")[:, tb * P:(tb + 1) * P],
                                        xdbl[:, tb * P:(tb + 1) * P], ident[:, :])
                last.then_inc(h_pe.sem, 1)

            def dt_proj(it, hf, j):
                if free := bank_free(it, f"dt{hf}_{j}"):
                    pe.wait_ge(*free)
                o = bank(f"dt{hf}_{j}").rearrange("p (c w) -> p c w", c=2)
                for c in range(2):
                    et = HT * hf + 2 * j + c
                    last = pe.matmul(o[:, c, :], wdt_sb[:, et * P:(et + 1) * P], xdbl[:, :],
                                     start=True, stop=True)
                last.then_inc(h_pe.sem, 1)

            def turn_skip(it, k, hf, tb):
                pe.wait_ge(h_act.sem, h_act.at(k, f"dd{hf}"))
                if free := bank_free(it, f"sd{hf}_{tb}"):
                    pe.wait_ge(*free)
                for e in range(HT):
                    last = pe.transpose(bank(f"sd{hf}_{tb}")[:, e * P:(e + 1) * P],
                                        ffn_mix[1][:, e, tb * P:(tb + 1) * P], ident[:, :])
                last.then_inc(h_pe.sem, 1)

            def turn_y(it, k, j):
                hf = j // 2
                if due(count := NSTT * k + TB * NS * (hf + 1)):
                    pe.wait_ge(y_added, count)
                if free := bank_free(it, f"YT{j}"):
                    pe.wait_ge(*free)
                o = bank(f"YT{j}").rearrange("p (c w) -> p c w", c=2)
                for c in range(2):
                    e = 2 * (j % 2) + c
                    for tb in range(TB):
                        last = pe.transpose(o[:, c, tb * P:(tb + 1) * P],
                                            y_rows[:, hf, tb, e * P:(e + 1) * P], ident[:, :])
                last.then_inc(y_pe.sem, 1)

            def out_proj(it, k, tb, part):
                if part == 0:
                    pe.wait_ge(y_dve.sem, y_dve.at(k, "g1"))
                    if free := bank_free(it, f"o{tb}"):
                        pe.wait_ge(*free)
                else:
                    pe.wait_ge(y_dve.sem, y_dve.at(k, "g3"))
                gated = (ffn_col[1], u[:, 1, :, :])[part]
                for e in range(HT):
                    last = pe.matmul(bank(f"o{tb}"), gated[:, e, tb * P:(tb + 1) * P],
                                     wout_sb[:, HT * part + e, :], start=part == 0 and e == 0,
                                     stop=part == 1 and e == HT - 1)
                if part == 1:
                    last.then_inc(y_pe.sem, 1)

            def turn_h(it, s, tb):
                if tb == 0:
                    if due(count := NSTEP * it + s + 1):
                        pe.wait_ge(scan_done, count)
                if due(count := NSTT * it + TB * (s - 2) + tb + 1):
                    pe.wait_ge(y_added, count)
                for e in range(HT):
                    last = pe.transpose(h_rows[:, s % 2, tb, e * P:(e + 1) * P],
                                        h[:, s % RING, e, tb, 1:SEG], ident[:, :])
                last.then_inc(h_turned, 1)

            def body(it, pair):
                scan, front, back = has(it, 0), has(it, 1), has(it, -1)
                f, b = it + 1, it - 1
                for s in range(NSTEP):
                    if scan:
                        turn_h(it, s, 0)
                        turn_h(it, s, 1)
                    if front and s == 0:
                        ffn_turn(it, 0, f)
                    if scan and s in (0, 1):
                        z(it, s)
                    if back and s == 2:
                        turn_y(it, b, 2)
                        turn_y(it, b, 3)
                    if front:
                        if s in (2, 3):
                            ffn_k(it, 0, f, s - 2)
                        if s in (4, 5):
                            ffn_r(it, 0, f, s - 4)
                    if scan and s in (6, 7):
                        dt_proj(it, 1, s - 6)
                    if front and s in (6, 7):
                        ffn_v(it, 0, f, s - 6)
                    if back and 8 <= s < 12:
                        out_proj(it, b, (s - 8) // 2, s % 2)
                    if scan and s in (12, 13):
                        z(it, s - 10)
                    if front and s == 13:
                        mamba_turn(it, f)
                    if scan and s == 14:
                        turn_skip(it, it, 1, 0)
                        turn_skip(it, it, 1, 1)
                    if front and s in (15, 16):
                        xs(it, f, s - 15)
                    if back and s == 17:
                        ffn_turn(it, 1, b)
                    if front and s in (18, 19):
                        xs(it, f, s - 16)
                    if back and s in (20, 21):
                        ffn_k(it, 1, b, s - 20)
                    if front:
                        if s in (22, 23):
                            xproj(it, f, s - 22)
                    if back and s == 24:
                        ffn_r(it, 1, b, 0)
                    if front and s == 25:
                        turn_c(it, f)
                    if front and s == 26:
                        dt_proj(it, 0, 0)
                        dt_proj(it, 0, 1)
                    if back:
                        if s == 26:
                            ffn_r(it, 1, b, 1)
                        if s in (27, 28):
                            ffn_v(it, 1, b, s - 27)
                    if scan and s == 30:
                        turn_y(it, it, 0)
                        turn_y(it, it, 1)
                    if front and s == 31:
                        turn_skip(it, f, 0, 0)
                        turn_skip(it, f, 0, 1)

            run(body, pe)

        @block.scalar
        def _(act):
            act.wait_ge(v_loaded, 16 * 9)
            act.activation(neg_a[:, :, :], neg_a[:, :, :], ACT.Exp).then_inc(init_act, 1)
            act.wait_ge(init_act, 1)
            act.activation(neg_a[:, :, :], neg_a[:, :, :], ACT.Copy, scale=-1.0).then_inc(init_act, 1)
            act.wait_ge(init_act, 2)
            act.wait_ge(init_dve, 3)
            act.wait_ge(init_pool, 11)

            def ffn_columns(i, k, pair):
                if i == 1:
                    act.wait_ge(y_pe.sem, y_pe.at(k, "o1"))
                if due(count := f_pe[i].at(k - 1, "v1")):
                    act.wait_ge(f_pe[i].sem, count)
                for j in range(2):
                    act.wait_ge(f_pe[i].sem, f_pe[i].at(k, f"T{j}"))
                    for_j = ffn_col[i][:, 2 * j:2 * j + 2, :].rearrange("p c (b s) -> p (c b) s", b=B)
                    act.activation(for_j[:, :, 1:SEG],
                                   bank(f"f{i}T{j}").rearrange("p (q t) -> p q t", t=T),
                                   ACT.Copy).then_inc(f_act[i].sem, 1)
                both = ffn_col[i][:, :, :].rearrange("p c (b s) -> p (c b) s", b=B)
                last = ffn_last[i][:, pair, :, :].rearrange("p c b -> p (c b)").unsqueeze(2)
                if due(count := f_act[i].at(k - 1, "last")):
                    act.wait_ge(f_act[i].sem, count)
                act.activation(both[:, :, 0:1], last, ACT.Copy).then_inc(f_act[i].sem, 1)
                act.wait_ge(f_act[i].sem, f_act[i].at(k, "lead"))
                act.activation(last, both[:, :, T:SEG], ACT.Copy).then_inc(f_act[i].sem, 1)

            def ffn_before(i, k, q, scanned=True, fronted=True):
                act.wait_ge(f_act[i].sem, f_act[i].at(k, "lead"))
                if i == 0:
                    if q == 1:
                        if due(count := f_pe[0].at(k - 1, "k1")):
                            act.wait_ge(f_pe[0].sem, count)
                        if due(count := f_pe[1].at(k - 3, "r1")):
                            act.wait_ge(f_pe[1].sem, count)
                    else:
                        if due(count := h_pe.at(k - 1, "sd0_1")):
                            act.wait_ge(h_pe.sem, count)
                elif q == 1:
                    act.wait_ge(h_pe.sem, h_pe.at(k + 1 if scanned else k, "sd1_1"))
                    if due(count := f_pe[1].at(k - 1, "k1")):
                        act.wait_ge(f_pe[1].sem, count)
                else:
                    if fronted:
                        act.wait_ge(f_pe[0].sem, f_pe[0].at(k + 2, "k1"))
                    if due(count := f_pe[1].at(k - 1, "r1")):
                        act.wait_ge(f_pe[1].sem, count)
                for ct in range(CT):
                    act.activation(col3(mix(i, q)[:, ct, :]), fcol(i, ct, 0), ACT.Copy,
                                   scale=vec[:, 2 + q, ct:ct + 1]).then_inc(f_act[i].sem, 1)

            def ffn_tanh(i, k, tb):
                act.wait_ge(f_pe[i].sem, f_pe[i].at(k, f"r{tb}"))
                act.activation(ffn_row[i][:, tb, :], bank(f"f{i}r{tb}"), ACT.Tanh,
                               scale=0.5).then_inc(f_act[i].sem, 1)

            def ffn_relu2(i, k, j):
                act.wait_ge(f_pe[i].sem, f_pe[i].at(k, f"k{j}"))
                act.wait_ge(f_dve[i].sem, f_dve[i].at(k, "xr3"))
                o = ffn_col[i][:, 2 * j:2 * j + 2, 0:W]
                act.activation(o, bank(f"f{i}k{j}").rearrange("p (c w) -> p c w", c=2),
                               ACT.Relu).then_inc(f_act[i].sem, 1)
                act.wait_ge(f_act[i].sem, f_act[i].at(k, f"rel{j}"))
                act.activation(o, o, ACT.Square).then_inc(f_act[i].sem, 1)

            def mamba_columns(k):
                if due(count := z_pe.at(k - 1, "3")):
                    act.wait_ge(z_pe.sem, count)
                for ct in range(CT):
                    if ct % 2 == 0:
                        act.wait_ge(m_pe.sem, m_pe.at(k, f"T{ct // 2}"))
                    act.activation(xn_col[:, ct, :], bank(f"mT{ct // 2}")[:, (ct % 2) * W:(ct % 2 + 1) * W],
                                   ACT.Identity, scale=vec[:, 4, ct:ct + 1],
                                   bias=vec[:, 5, ct:ct + 1]).then_inc(m_act.sem, 1)

            def conv_start(k, j, pair):
                act.wait_ge(m_pe.sem, m_pe.at(k, f"xs{j}"))
                if j >= 2:
                    act.wait_ge(m_dve.sem, m_dve.at(k, f"c2b{j - 2}"))
                else:
                    if due(count := m_dve.at(k - 1, f"c2b{j + 2}")):
                        act.wait_ge(m_dve.sem, count)
                pad = xs_pad[:, j % 2, :, :, :].rearrange("p c b s -> p (c b) s")
                hist = xs_last[:, pair, 2 * j:2 * j + 2, :, :].rearrange("p c b s -> p (c b) s")
                src = bank(f"xs{j}")
                act.activation(pad[:, :, KC - 1:], src.rearrange("p (q t) -> p q t", t=T),
                               ACT.Copy).then_inc(m_act.sem, 1)
                if due(count := m_act.at(k - 1, f"last{j}")):
                    act.wait_ge(m_act.sem, count)
                act.activation(pad[:, :, 0:KC - 1], hist, ACT.Copy).then_inc(m_act.sem, 1)
                act.wait_ge(m_act.sem, m_act.at(k, f"lead{j}"))
                act.activation(hist, pad[:, :, T:T + KC - 1], ACT.Copy).then_inc(m_act.sem, 1)
                if due(count := h_pool.at(k - 1, "u1")):
                    act.wait_ge(h_pool.sem, count)
                if due(count := h_act.at(k - 1, "dd1")):
                    act.wait_ge(h_act.sem, count)
                for c in range(2):
                    et = 2 * j + c
                    act.activation(xc2[:, et, :], src[:, c * W:(c + 1) * W], ACT.Identity,
                                   scale=conv_sb[:, et, KC - 1:KC],
                                   bias=evec[:, 0, et:et + 1]).then_inc(m_act.sem, 1)

            def conv_tanh(k, j):
                act.wait_ge(m_dve.sem, m_dve.at(k, f"c2b{j}"))
                if due(count := m_dve.at(k, f"silu{j - 2}") if j >= 2 else m_dve.at(k - 1, f"silu{j + 2}")):
                    act.wait_ge(m_dve.sem, count)
                act.activation(th[:, j % 2, :], xc2[:, 2 * j:2 * j + 2, :].rearrange("p c w -> p (c w)"),
                               ACT.Tanh, scale=0.5).then_inc(m_act.sem, 1)

            def x_rows(k):
                act.wait_ge(m_pe.sem, m_pe.at(k, "xp"))
                if due(count := h_pe.at(k - 1, "dt1_1")):
                    act.wait_ge(h_pe.sem, count)
                if due(count := 16 * k):
                    act.wait_ge(b_stored, count)
                act.activation(xdbl[0:XR, :], bank("xp")[0:XR, 0:W], ACT.Copy,
                               scale=xscale[:, 0:1]).then_inc(m_act.sem, 1)

            def keep_c(k, pair):
                act.wait_ge(h_pe.sem, h_pe.at(k, "C"))
                if due(count := NSTT * (k - 1)):
                    act.wait_ge(y_added, count)
                act.activation(c_rows[:, pair, :, :],
                               bank("C").rearrange("p (q c) -> p q c", c=P)[:, 0:TB, R + NS:XR],
                               ACT.Copy).then_inc(h_act.sem, 1)

            def softplus_x(k, hf, j):
                if j == 0:
                    if due(count := NEXP * (k - 1) + NEXP // 2 * (hf + 1)):
                        act.wait_ge(decay_done, count)
                act.wait_ge(h_pe.sem, h_pe.at(k, f"dt{hf}_{j}"))
                for e in (2 * j, 2 * j + 1):
                    act.activation(delta[:, hf, e, :], bank(f"dt{hf}_{j}")[:, (e % 2) * W:(e % 2 + 1) * W],
                                   ACT.Identity,
                                   bias=evec[:, 1, HT * hf + e:HT * hf + e + 1]).then_inc(h_act.sem, 1)

            def softplus_exp(k, hf):
                if hf == 0:
                    if due(count := 2 * NSTEP * (k - 1) + NSTEP):
                        act.wait_ge(dbx_done, count)
                else:
                    if due(count := f_dve[1].at(k - 2, "o1")):
                        act.wait_ge(f_dve[1].sem, count)
                    if due(count := h_dve.at(k - 1, "delta1")):
                        act.wait_ge(h_dve.sem, count)
                act.wait_ge(h_act.sem, h_act.at(k, f"xd{hf}"))
                act.activation(soft(hf), delta[:, hf, :, :].rearrange("p e w -> p (e w)"),
                               ACT.Abs).then_inc(h_act.sem, 1)
                act.wait_ge(h_act.sem, h_act.at(k, f"abs{hf}"))
                act.activation(soft(hf), soft(hf), ACT.Exp, scale=-1.0).then_inc(h_act.sem, 1)

            def softplus_ln(k, hf):
                act.wait_ge(h_act.sem, h_act.at(k, f"exp{hf}"))
                act.activation(soft(hf), soft(hf), ACT.Ln, bias=1.0).then_inc(h_act.sem, 1)

            def skip_columns(k, hf, fronted=True):
                if hf == 0:
                    act.wait_ge(f_pe[0].sem, f_pe[0].at(k, "r1"))
                    if due(count := f_pe[1].at(k - 2, "k1")):
                        act.wait_ge(f_pe[1].sem, count)
                    if due(count := h_pe.at(k - 1, "sd1_1")):
                        act.wait_ge(h_pe.sem, count)
                else:
                    if fronted:
                        act.wait_ge(f_pe[0].sem, f_pe[0].at(k + 1, "r1"))
                    act.wait_ge(h_pe.sem, h_pe.at(k, "sd0_1"))
                for e in range(HT):
                    et = HT * hf + e
                    act.activation(ffn_mix[1][:, e, :], xc2[:, et, :], ACT.Copy,
                                   scale=evec[:, 3, et:et + 1]).then_inc(h_act.sem, 1)

            def skip_rows(k, hf, tb):
                act.wait_ge(h_pe.sem, h_pe.at(k, f"sd{hf}_{tb}"))
                if due(count := y_pe.at(k - 1, f"T{2 * hf + 1}")):
                    act.wait_ge(y_pe.sem, count)
                act.activation(y_rows[:, hf, tb, :], bank(f"sd{hf}_{tb}"), ACT.Copy).then_inc(h_act.sem, 1)

            def gate_tanh(k, j):
                act.wait_ge(z_pe.sem, z_pe.at(k, f"{j}"))
                if due(count := z_dve.at(k, "0") + j - 1):
                    act.wait_ge(z_dve.sem, count)
                act.activation(zth[:, :], bank(f"z{j}"), ACT.Tanh, scale=0.5).then_inc(z_act.sem, 1)

            def decays(it, s):
                hf, n = divmod(s, NS)
                act.wait_ge(h_dve.sem, h_dve.at(it, f"delta{hf}"))
                if due(count := NSTEP * it + s - 1):
                    act.wait_ge(scan_done, count)
                for e in range(HT):
                    act.activation(decay[:, s % 2, e, :, 1:SEG], col3(delta[:, hf, e, :]), ACT.Exp,
                                   scale=neg_a[:, HT * hf + e, n:n + 1]).then_inc(decay_done, 1)

            def save(it, s, pair):
                if due(count := NSTEP * it + s + 1):
                    act.wait_ge(scan_done, count)
                if due(count := 2 * NSTEP * it + 2 * s + 1):
                    act.wait_ge(dbx_done, count)
                act.activation(state[:, pair, s, :, :], h[:, s % RING, :, :, T], ACT.Copy).then_inc(saved, 1)

            def body(it, pair):
                scan, front, back = has(it, 0), has(it, 1), has(it, -1)
                f, b = it + 1, it - 1
                other = (pair + 1) % PAIRS
                for s in range(NSTEP):
                    if scan:
                        decays(it, s)
                    if s < SAVE:
                        if back:
                            save(b, NSTEP - SAVE + s, other)
                    elif scan:
                        save(it, s - SAVE, pair)
                    if scan and s == 2:
                        skip_rows(it, 0, 0)
                        skip_rows(it, 0, 1)
                    if front:
                        if s == 3:
                            ffn_columns(0, f, other)
                            ffn_before(0, f, 1)
                        if s == 4:
                            ffn_before(0, f, 0)
                    if scan and s in (4, 5):
                        gate_tanh(it, s - 4)
                    if front:
                        if s in (6, 7):
                            ffn_relu2(0, f, s - 6)
                        if s in (8, 9):
                            ffn_tanh(0, f, s - 8)
                    if scan:
                        if s == 10:
                            softplus_x(it, 1, 0)
                        if s == 11:
                            softplus_x(it, 1, 1)
                            softplus_exp(it, 1)
                        if s == 12:
                            softplus_ln(it, 1)
                        if s == 13:
                            skip_columns(it, 1, front)
                        if s in (15, 16):
                            gate_tanh(it, s - 13)
                    if front and s == 16:
                        mamba_columns(f)
                    if scan and s == 17:
                        skip_rows(it, 1, 0)
                        skip_rows(it, 1, 1)
                    if front:
                        if s == 18:
                            conv_start(f, 0, other)
                        if s == 19:
                            conv_start(f, 1, other)
                        if s == 20:
                            conv_tanh(f, 0)
                    if back and s == 20:
                        ffn_columns(1, b, other)
                        ffn_before(1, b, 1, scan, front)
                    if front:
                        if s == 21:
                            conv_start(f, 2, other)
                            conv_tanh(f, 1)
                        if s == 22:
                            conv_start(f, 3, other)
                    if back and s == 22:
                        ffn_before(1, b, 0, scan, front)
                    if front and s in (23, 24):
                        conv_tanh(f, s - 21)
                    if back and s in (23, 24):
                        ffn_relu2(1, b, s - 23)
                    if front:
                        if s == 26:
                            x_rows(f)
                        if s == 27:
                            keep_c(f, other)
                    if back and s == 27:
                        ffn_tanh(1, b, 0)
                    if front:
                        if s == 28:
                            softplus_x(f, 0, 0)
                            softplus_x(f, 0, 1)
                        if s == 29:
                            softplus_exp(f, 0)
                    if back and s == 29:
                        ffn_tanh(1, b, 1)
                    if front:
                        if s == 30:
                            softplus_ln(f, 0)
                        if s == 31:
                            skip_columns(f, 0)
            run(body, act)

        @block.vector
        def _(dve):
            dve.memset(decay[:, :, :, :, :], 0.0).then_inc(init_dve, 1)
            dve.wait_ge(v_loaded, 16 * 9)
            dve.tensor_scalar(vec[:, 2:4, :], vec[:, 0:2, :], -1.0, 1.0, ALU.mult,
                              ALU.add).then_inc(init_dve, 1)
            dve.tensor_scalar(evec[:, 3, :], evec[:, 2, :], 0.5, None, ALU.mult).then_inc(init_dve, 1)
            dve.wait_ge(init_dve, 3)

            def norm_stats(q, marks, k, src):
                for tb in range(TB):
                    dve.bn_stats(stats[q][:, tb, :], src[:, tb, :]).then_inc(marks.sem, 1)
                for tb in range(TB):
                    dve.wait_ge(marks.sem, marks.at(k, f"st{tb}"))
                    dve.sem_inc(passed_dve, 1)
                    dve.bn_aggr(mv[q][:, tb, :], stats[q][:, tb, :]).then_inc(marks.sem, 1)

            def normalise(q, pool_marks, marks, k, src, dst, r0):
                dve.wait_ge(pool_marks.sem, pool_marks.at(k, f"y{NEWTON - 1}"))
                for tb in range(TB):
                    dve.tensor_scalar(dst[:, tb, :], src[:, tb, :], mv[q][:, tb, 0:1],
                                      rs[q][:, r0 + tb:r0 + tb + 1], ALU.subtract,
                                      ALU.mult).then_inc(marks.sem, 1)

            def ffn_stats(i, k, src):
                if due(count := f_pool[i].at(k - 1, "v")):
                    dve.wait_ge(f_pool[i].sem, count)
                norm_stats(i, f_dve[i], k, src)

            def ffn_norm(i, k, src, scanned=True):
                if i == 0:
                    if due(count := m_pe.at(k - 1, "T1")):
                        dve.wait_ge(m_pe.sem, count)
                else:
                    if due(count := f_dve[i].at(k - 1, "o1")):
                        dve.wait_ge(f_dve[i].sem, count)
                    if due(count := h_dve.at(k + 1 if scanned else k, "delta1")):
                        dve.wait_ge(h_dve.sem, count)
                normalise(i, f_pool[i], f_dve[i], k, src, ffn_row[i], 0)

            def ffn_mix_in(i, k, q):
                for ct in range(CT):
                    dve.wait_ge(f_act[i].sem, f_act[i].at(k, f"{'pr' if q == 0 else 'pk'}{ct}"))
                    m = col3(mix(i, q)[:, ct, :])
                    dve.scalar_tensor_tensor(out=m, in0=fcol(i, ct, 1), scalar=vec[:, q, ct:ct + 1],
                                             in1=m, op0=ALU.mult, op1=ALU.add).then_inc(f_dve[i].sem, 1)

            def ffn_gate(i, k, tb):
                dve.wait_ge(f_pe[i].sem, f_pe[i].at(k, f"v{tb}"))
                dve.wait_ge(f_act[i].sem, f_act[i].at(k, f"th{tb}"))
                g = ffn_row[i][:, tb, :]
                dve.scalar_tensor_tensor(out=g, in0=g, scalar=1.0, in1=bank(f"f{i}v{tb}"), op0=ALU.add,
                                         op1=ALU.mult).then_inc(f_dve[i].sem, 1)

            def ffn_add(i, k, tb, xx):
                dve.wait_ge(f_dve[i].sem, f_dve[i].at(k, f"g{tb}"))
                dve.scalar_tensor_tensor(out=xx[:, tb, :], in0=ffn_row[i][:, tb, :], scalar=0.25,
                                         in1=xx[:, tb, :], op0=ALU.mult,
                                         op1=ALU.add).then_inc(f_dve[i].sem, 1)

            def mamba_norm(k, pair):
                if due(count := y_dve.at(k - 2, "x1")):
                    dve.wait_ge(y_dve.sem, count)
                normalise(2, m_pool, m_dve, k, xin, res[:, pair, :, :], 0)
                normalise(2, m_pool, m_dve, k, xin, ffn_row[0], TB)

            def conv_taps(k, j):
                for q in range(KC - 1):
                    for c in range(2):
                        et = 2 * j + c
                        if q == 0:
                            dve.wait_ge(m_act.sem, m_act.at(k, f"tap{'ab'[c]}{j}"))
                        else:
                            dve.wait_ge(m_dve.sem, m_dve.at(k, f"c{q - 1}{'ab'[c]}{j}"))
                        o = col3(xc2[:, et, :])
                        dve.scalar_tensor_tensor(out=o, in0=xs_pad[:, j % 2, c, :, q:q + T],
                                                 scalar=conv_sb[:, et, q:q + 1], in1=o, op0=ALU.mult,
                                                 op1=ALU.add).then_inc(m_dve.sem, 1)

            def conv_silu(k, j):
                dve.wait_ge(m_act.sem, m_act.at(k, f"th{j}"))
                o = xc2[:, 2 * j:2 * j + 2, :].rearrange("p c w -> p (c w)")
                dve.scalar_tensor_tensor(out=o, in0=th[:, j % 2, :], scalar=1.0, in1=o, op0=ALU.add,
                                         op1=ALU.mult).then_inc(m_dve.sem, 1)

            def softplus_sum(k, hf):
                dve.wait_ge(h_act.sem, h_act.at(k, f"ln{hf}"))
                d = delta[:, hf, :, :].rearrange("p e w -> p (e w)")
                dve.scalar_tensor_tensor(out=d, in0=d, scalar=0.0,
                                         in1=soft(hf), op0=ALU.max,
                                         op1=ALU.add).then_inc(h_dve.sem, 1)

            def gate_silu(k, j):
                dve.wait_ge(z_act.sem, z_act.at(k, f"{j}"))
                if due(count := y_dve.at(k - 1, f"g{j}")):
                    dve.wait_ge(y_dve.sem, count)
                dve.scalar_tensor_tensor(out=gate[:, 2 * j:2 * j + 2, :].rearrange("p c w -> p (c w)"),
                                         in0=zth[:, :], scalar=1.0, in1=bank(f"z{j}"), op0=ALU.add,
                                         op1=ALU.mult).then_inc(z_dve.sem, 1)

            def gate_y(k, j):
                dve.wait_ge(y_pe.sem, y_pe.at(k, f"T{j}"))
                dve.wait_ge(z_dve.sem, z_dve.at(k, f"{j}"))
                if j < 2:
                    if due(count := f_pe[1].at(k - 1, "v1")):
                        dve.wait_ge(f_pe[1].sem, count)
                    o = ffn_col[1][:, 2 * j:2 * j + 2, 0:W]
                else:
                    if due(count := 2 * NSTEP * (k + 1)):
                        dve.wait_ge(dbx_done, count)
                    o = u[:, 1, 2 * j - HT:2 * j - HT + 2, :]
                dve.tensor_tensor(o, gate[:, 2 * j:2 * j + 2, :],
                                  bank(f"YT{j}").rearrange("p (c w) -> p c w", c=2),
                                  ALU.mult).then_inc(y_dve.sem, 1)

            def out_add(k, tb, pair):
                dve.wait_ge(y_pe.sem, y_pe.at(k, f"o{tb}"))
                dve.wait_ge(m_pool.sem, m_pool.at(k, "res"))
                if due(count := 16 * TB * k):
                    dve.wait_ge(out_stored, count)
                dve.scalar_tensor_tensor(out=xout[:, tb, :], in0=bank(f"o{tb}"), scalar=0.5,
                                         in1=res[:, pair, tb, :], op0=ALU.mult,
                                         op1=ALU.add).then_inc(y_dve.sem, 1)

            def scan(it, s):
                if due(count := 2 * NSTEP * it + 2 * s + 2):
                    dve.wait_ge(dbx_done, count)
                if due(count := NEXP * it + HT * (s + 1)):
                    dve.wait_ge(decay_done, count)
                hs = h[:, s % RING, :, :, :].rearrange("p e b s -> p (e b s)")
                dve.tensor_tensor_scan(hs, decay[:, s % 2, :, :, :].rearrange("p e b s -> p (e b s)"),
                                       hs, 0.0, ALU.mult, ALU.add).then_inc(scan_done, 1)

            def add_y(it, s, tb, pair):
                hf, n = divmod(s, NS)
                if due(count := NSTT * it + TB * s + tb + 1):
                    dve.wait_ge(h_turned, count)
                if n == 0:
                    dve.wait_ge(h_act.sem, h_act.at(it, f"yb{hf}"))
                else:
                    if due(count := NSTT * it + TB * (s - 1) + tb + 1):
                        dve.wait_ge(y_added, count)
                yy = y_rows[:, hf, tb, :]
                dve.scalar_tensor_tensor(out=yy, in0=h_rows[:, s % 2, tb, :],
                                         scalar=c_rows[:, pair, tb, n:n + 1],
                                         in1=yy, op0=ALU.mult, op1=ALU.add).then_inc(y_added, 1)

            def body(it, pair):
                scn, front, back, ahead = has(it, 0), has(it, 1), has(it, -1), has(it, 2)
                f, b = it + 1, it - 1
                other = (pair + 1) % PAIRS
                for s in range(NSTEP):
                    if scn:
                        scan(it, s)
                    for tb in range(TB):
                        if s < LAG:
                            if back:
                                add_y(b, NSTEP - LAG + s, tb, other)
                        elif scn:
                            add_y(it, s - LAG, tb, pair)
                    if back and s == 0:
                        gate_y(b, 0)
                        gate_y(b, 1)
                    if front:
                        if s == 2:
                            ffn_mix_in(0, f, 1)
                        if s == 3:
                            ffn_mix_in(0, f, 0)
                    if scn and s == 3:
                        gate_silu(it, 0)
                    if back and s == 3:
                        gate_y(b, 2)
                        gate_y(b, 3)
                    if scn and s == 5:
                        gate_silu(it, 1)
                    if front:
                        if s == 8:
                            ffn_gate(0, f, 0)
                        if s == 9:
                            ffn_gate(0, f, 1)
                            ffn_add(0, f, 0, xin)
                            ffn_add(0, f, 1, xin)
                            dve.wait_ge(f_dve[0].sem, f_dve[0].at(f, "o1"))
                            if due(count := m_pool.at(f - 1, "v2")):
                                dve.wait_ge(m_pool.sem, count)
                            norm_stats(2, m_dve, f, xin)
                    if back and s == 11:
                        out_add(b, 0, other)
                    if scn and s == 11:
                        softplus_sum(it, 1)
                    if back and s == 13:
                        out_add(b, 1, other)
                    if front and s == 13:
                        mamba_norm(f, other)
                    if back and s == 13:
                        dve.wait_ge(y_dve.sem, y_dve.at(b, "x1"))
                        ffn_stats(1, b, xout)
                    if scn and s in (14, 15):
                        gate_silu(it, s - 12)
                    if back and s == 16:
                        ffn_norm(1, b, xout, scn)
                    if front:
                        if s == 17:
                            conv_taps(f, 0)
                        if s == 18:
                            conv_taps(f, 1)
                        if s == 19:
                            conv_silu(f, 0)
                    if back and s == 19:
                        ffn_mix_in(1, b, 1)
                    if back and s == 21:
                        ffn_mix_in(1, b, 0)
                    if front:
                        if s == 20:
                            conv_silu(f, 1)
                            conv_taps(f, 2)
                        if s == 21:
                            conv_taps(f, 3)
                        if s == 22:
                            conv_silu(f, 2)
                        if s == 23:
                            conv_silu(f, 3)
                    if ahead and s == 25:
                        dve.wait_ge(x_loaded, (it + 3) * (16 * TB))
                        ffn_stats(0, it + 2, xin)
                    if front and s == 29:
                        softplus_sum(f, 0)
                    if back:
                        if s == 28:
                            ffn_gate(1, b, 0)
                        if s == 29:
                            ffn_gate(1, b, 1)
                            ffn_add(1, b, 0, xout)
                            ffn_add(1, b, 1, xout)
                    if ahead and s == 30:
                        ffn_norm(0, it + 2, xin)

            run(body, dve)

        @block.gpsimd
        def _(pool):
            pool.memset(ident[:, :], 0.0).then_inc(init_pool, 1)
            pool.memset(wdt_sb[:, :], 0.0).then_inc(init_pool, 1)
            pool.wait_ge(init_pool, 1)
            pool.affine_select(out=ident[:, :], in_=ident[:, :], compare_op=ALU.not_equal, fill=1.0,
                               base=0, pattern=[[-1, P]], channel_multiplier=1).then_inc(init_pool, 1)
            pool.memset(xdbl[:, :], 0.0).then_inc(init_pool, 1)
            pool.memset(state[:, :, :, :, :], 0.0).then_inc(init_pool, 1)
            pool.memset(xs_last[:, :, :, :, :], 0.0).then_inc(init_pool, 1)
            for i in range(2):
                pool.memset(ffn_last[i][:, :, :, :], 0.0).then_inc(init_pool, 1)
            pool.memset(xscale[:, :], 0.5).then_inc(init_pool, 1)
            pool.wait_ge(init_pool, 9)
            pool.affine_select(out=xscale[:, :], in_=xscale[:, :], compare_op=ALU.is_gt, fill=0.25,
                               base=R, pattern=[[0, 1]], channel_multiplier=-1).then_inc(init_pool, 1)
            pool.wait_ge(init_pool, 10)
            pool.affine_select(out=xscale[:, :], in_=xscale[:, :], compare_op=ALU.is_gt, fill=0.5,
                               base=R + NS, pattern=[[0, 1]], channel_multiplier=-1).then_inc(init_pool, 1)
            pool.wait_ge(init_pool, 11)

            def rsqrt(q, marks, k, n):
                v, t, y = nv[q][:, 0:n], nt[q][:, 0:n], rs[q][:, 0:n]
                pool.wait_ge(marks.sem, marks.at(k, marks.names[marks.names.index("guess") - 1]))
                pool.sem_inc(passed_pool, 1)
                pool.tensor_scalar(y.bitcast(I32), v.bitcast(I32), -0.5, RSQRT_GUESS, ALU.mult,
                                   ALU.add).then_inc(marks.sem, 1)
                before = "guess"
                for i in range(NEWTON):
                    pool.wait_ge(marks.sem, marks.at(k, before))
                    pool.tensor_tensor(t, y, y, ALU.mult).then_inc(marks.sem, 1)
                    pool.wait_ge(marks.sem, marks.at(k, f"yy{i}"))
                    pool.tensor_tensor(t, t, v, ALU.mult).then_inc(marks.sem, 1)
                    pool.wait_ge(marks.sem, marks.at(k, f"vyy{i}"))
                    pool.sem_inc(passed_pool, 1)
                    pool.tensor_scalar(t, t, -0.5, 1.5, ALU.mult, ALU.add).then_inc(marks.sem, 1)
                    pool.wait_ge(marks.sem, marks.at(k, f"half{i}"))
                    pool.tensor_tensor(y, y, t, ALU.mult).then_inc(marks.sem, 1)
                    before = f"y{i}"

            def ffn_rstd(i, k):
                if due(count := f_dve[i].at(k - 1, "ln1")):
                    pool.wait_ge(f_dve[i].sem, count)
                pool.wait_ge(f_dve[i].sem, f_dve[i].at(k, "mv1"))
                pool.sem_inc(passed_pool, 1)
                pool.tensor_scalar(nv[i][:, 0:TB], mv[i][:, :, 1], 1.0, EPS, ALU.mult,
                                   ALU.add).then_inc(f_pool[i].sem, 1)
                rsqrt(i, f_pool[i], k, TB)

            def mamba_rstd(k):
                if due(count := m_dve.at(k - 1, "in1")):
                    pool.wait_ge(m_dve.sem, count)
                pool.wait_ge(m_dve.sem, m_dve.at(k, "mv1"))
                pool.sem_inc(passed_pool, 1)
                pool.tensor_scalar(nv[2][:, 0:TB], mv[2][:, :, 1], 1.0, EPS, ALU.mult,
                                   ALU.add).then_inc(m_pool.sem, 1)
                pool.tensor_scalar(nv[2][:, TB:2 * TB], mv[2][:, :, 1], 1.0 + EPS, EPS * EPS, ALU.mult,
                                   ALU.add).then_inc(m_pool.sem, 1)
                rsqrt(2, m_pool, k, 2 * TB)

            def make_res(k, pair):
                pool.wait_ge(m_dve.sem, m_dve.at(k, "ln1"))
                pool.tensor_tensor(res[:, pair, :, :], res[:, pair, :, :], xin[:, :, :], ALU.add).then_inc(m_pool.sem, 1)

            def make_u(k, hf):
                pool.wait_ge(h_dve.sem, h_dve.at(k, f"delta{hf}"))
                pool.wait_ge(m_dve.sem, m_dve.at(k, "silu3"))
                if hf == 1:
                    if due(count := y_pe.at(k - 1, "o1")):
                        pool.wait_ge(y_pe.sem, count)
                pool.tensor_tensor(u[:, hf, :, :], delta[:, hf, :, :], xc2[:, HT * hf:HT * (hf + 1), :],
                                   ALU.mult).then_inc(h_pool.sem, 1)

            def products(it, s, pair):
                hf, n = divmod(s, NS)
                if due(count := NSTT * it + TB * (s - RING + 1)):
                    pool.wait_ge(h_turned, count)
                    pool.sem_inc(passed_pool, 1)
                if due(count := NSTEP * it + s - RING + 1):
                    pool.wait_ge(saved, count)
                    pool.sem_inc(passed_pool, 1)
                pool.tensor_copy(h[:, s % RING, :, :, 0], state[:, pair, s, :, :]).then_inc(dbx_done, 1)
                j = s // NBG
                if s % NBG == 0:
                    pool.wait_ge(b_loaded[j % 2], it * (16 * NG // 2) + 16 * (j // 2 + 1))
                if n == 0:
                    pool.wait_ge(h_pool.sem, h_pool.at(it, f"u{hf}"))
                bb = b_all[:, j % 2, s % NBG, :].rearrange("p (b t) -> p b t", b=B)
                pool.tensor_tensor(h[:, s % RING, :, :, 1:SEG],
                                   u[:, hf, :, :].rearrange("p e (b t) -> p e b t", b=B),
                                   bb.unsqueeze(1).broadcast_to([P, HT, B, T]),
                                   ALU.mult).then_inc(dbx_done, 1)

            def body(it, pair):
                scn, front, back, ahead = has(it, 0), has(it, 1), has(it, -1), has(it, 2)
                f, b = it + 1, it - 1
                for s in range(NSTEP):
                    if scn:
                        products(it, s, pair)
                    if front and s == 12:
                        mamba_rstd(f)
                    if scn and s == 14:
                        make_u(it, 1)
                    if back and s == 15:
                        ffn_rstd(1, b)
                    if front and s == 18:
                        make_res(f, (pair + 1) % PAIRS)
                    if ahead and s == 27:
                        ffn_rstd(0, it + 2)
                    if front and s == 31:
                        make_u(f, 0)

            run(body, pool)


def kernel(L0_attn_x, L0_attn_ln_w, L0_attn_ln_b, L0_attn_W_in, L0_attn_W_conv, L0_attn_b_conv,
           L0_attn_W_xproj, L0_attn_W_dt, L0_attn_b_dt, L0_attn_A_log, L0_attn_D_skip, L0_attn_W_out,
           L0_ffn_W_r, L0_ffn_W_k, L0_ffn_W_v, L0_ffn_mu_r, L0_ffn_mu_k):
    import numpy as np
    import concourse.bacc as bacc
    from concourse.bass_utils import run_bass_kernel_spmd

    def by_tile(v):
        return np.asarray(v).reshape(-1, P).T

    arrays = {
        "x": L0_attn_x, "mu_r": by_tile(L0_ffn_mu_r), "mu_k": by_tile(L0_ffn_mu_k),
        "w_r": np.asarray(L0_ffn_W_r).T, "w_k": np.asarray(L0_ffn_W_k).T,
        "w_v": np.asarray(L0_ffn_W_v).T, "ln_w": by_tile(L0_attn_ln_w), "ln_b": by_tile(L0_attn_ln_b),
        "w_in": np.asarray(L0_attn_W_in).T, "w_conv": L0_attn_W_conv, "b_conv": by_tile(L0_attn_b_conv),
        "w_x": np.asarray(L0_attn_W_xproj).T, "w_dt": np.asarray(L0_attn_W_dt).T,
        "b_dt": by_tile(L0_attn_b_dt), "a_log": L0_attn_A_log, "d_skip": by_tile(L0_attn_D_skip),
        "w_out": np.asarray(L0_attn_W_out).T,
    }
    arrays = {f"in_{n}": np.ascontiguousarray(a) for n, a in arrays.items()}
    nc = bacc.Bacc("TRN2", target_bir_lowering=False, num_devices=1)
    args = [nc.dram_tensor(n, a.shape, mybir.dt.from_np(a.dtype), kind="ExternalInput").ap()
            for n, a in arrays.items()]
    out = nc.dram_tensor("out_0", tuple(L0_attn_x.shape), F32, kind="ExternalOutput").ap()
    build(nc, *args, out)
    r = run_bass_kernel_spmd(nc, [arrays], core_ids=[0])
    return r.results[0]["out_0"]
```

```python
from contextlib import ExitStack

import concourse.bass as bass
from concourse import mybir

ALU = mybir.AluOpType
ACT = mybir.ActivationFunctionType
F32 = mybir.dt.float32
I32 = mybir.dt.int32

P = 128
T = 128
SEG = T + 1
EPS = 1e-5
RSQRT_GUESS = 1597463007.0
NEWTON = 3


class Marks:

    def __init__(self, sem, names):
        self.sem, self.names = sem, names.split() if isinstance(names, str) else names
        assert len(set(self.names)) == len(self.names)

    def at(self, chunk, name):
        return chunk * len(self.names) + (self.names.index(name) + 1)


def due(value):
    return not isinstance(value, int) or value > 0


def build(nc, x, mu_r, mu_k, w_r, w_k, w_v, ln_w, ln_b, w_in, w_conv, b_conv, w_x, w_dt, b_dt,
          a_log, d_skip, w_out, out):
    BATCHES, L, D = x.shape
    E, NS = a_log.shape
    R = w_dt.shape[0]
    KC = w_conv.shape[1]
    B = 2
    PAIRS = BATCHES // B
    NCH = L // T * PAIRS
    W = B * T
    CT, ET = D // P, E // P
    HT = ET // 2
    TB = W // P
    NSTEP = 2 * NS
    XR = R + 2 * NS
    NEXP, NSTT = NSTEP * HT, NSTEP * TB
    RING = 4
    LAG = 2
    SAVE = 3
    BANKS = 4
    NBG = 2
    NG = NSTEP // NBG
    assert TB == 2 and CT == 4 and HT == 4 and T == P and PAIRS == 2 and R == 32 and NS == 16 and XR == 64

    with ExitStack() as ctx:
        def sb(name, shape, dt=F32):
            return ctx.enter_context(nc.sbuf_tensor(name, shape, dt))

        def ps(name, shape):
            return ctx.enter_context(nc.psum_tensor(name, shape, F32))

        def sem(name):
            return ctx.enter_context(nc.semaphore(name))

        h_rows = ps("h_rows", [P, 2, TB, 512])
        mm = ps("mm", [P, BANKS, 512])

        wr_sb, wk_sb, wv_sb = (sb(n, [P, CT, D]) for n in ("wr_sb", "wk_sb", "wv_sb"))
        win_sb = sb("win_sb", [P, CT, 2 * E])
        wx_sb = sb("wx_sb", [P, ET, XR])
        wdt_sb = sb("wdt_sb", [P, E])
        wout_sb = sb("wout_sb", [P, ET, D])
        ident = sb("ident", [P, P])
        vec = sb("vec", [P, 6, CT])
        conv_sb = sb("conv_sb", [P, ET, KC])
        evec = sb("evec", [P, 4, ET])
        neg_a = sb("neg_a", [P, ET, NS])
        xscale = sb("xscale", [XR, 1])

        xin = sb("xin", [P, TB, D])
        res = sb("res", [P, PAIRS, TB, D])
        xout = sb("xout", [P, TB, D])
        ffn_row = [sb(f"ffn_row{i}", [P, TB, D]) for i in range(2)]
        ffn_col = [sb(f"ffn_col{i}", [P, CT, B * SEG]) for i in range(2)]
        ffn_mix = [sb(f"ffn_mix{i}", [P, CT, W]) for i in range(2)]
        ffn_last = [sb(f"ffn_last{i}", [P, PAIRS, CT, B]) for i in range(2)]
        stats = [sb(f"stats{i}", [P, TB, 6]) for i in range(3)]
        mv = [sb(f"mv{i}", [P, TB, 2]) for i in range(3)]
        nv = [sb(f"nv{i}", [P, 2 * TB]) for i in range(3)]
        shift = [sb(f"shift{i}", [P, TB]) for i in range(2)]
        nt = [sb(f"nt{i}", [P, 2 * TB]) for i in range(3)]
        rs = [sb(f"rs{i}", [P, 2 * TB]) for i in range(3)]
        xn_col = sb("xn_col", [P, PAIRS, CT, W])
        xs_pad = sb("xs_pad", [P, 2, 2, B, T + KC - 1])
        xs_last = sb("xs_last", [P, PAIRS, ET, B, KC - 1])
        xc2 = sb("xc2", [P, ET, W])
        gate = sb("gate", [P, ET, W])
        xdbl = sb("xdbl", [P, W])
        c_rows = sb("c_rows", [P, PAIRS, TB, NS])
        delta = sb("delta", [P, 2, HT, W])
        u = sb("u", [P, 2, HT, W])
        b_all = sb("b_all", [P, 2, NBG, W])
        decay = sb("decay", [P, 2, HT, B, SEG])
        h = sb("h", [P, RING, HT, B, SEG])
        state = sb("state", [P, PAIRS, NSTEP, HT, B])
        y_rows = sb("y_rows", [P, 2, TB, 512])

        b_dram = nc.dram_tensor("b_scratch", (NCH, NS * W), F32).ap()

        v_loaded = sem("v_loaded")
        wk_loaded, wr_loaded, wv_loaded = sem("wk_loaded"), sem("wr_loaded"), sem("wv_loaded")
        win_loaded, wx_loaded = sem("win_loaded"), sem("wx_loaded")
        wdt_loaded, wout_loaded = sem("wdt_loaded"), sem("wout_loaded")
        x_loaded, out_stored = sem("x_loaded"), sem("out_stored")
        b_stored = sem("b_stored")
        b_loaded = [sem("b_loaded0"), sem("b_loaded1")]
        init_pool, init_dve, init_act = sem("init_pool"), sem("init_dve"), sem("init_act")

        passed_sp, passed_dve, passed_pool = sem("passed_sp"), sem("passed_dve"), sem("passed_pool")

        decay_done = sem("decay_done")
        dbx_done = sem("dbx_done")
        scan_done = sem("scan_done")
        saved = sem("saved")
        h_turned = sem("h_turned")
        y_added = sem("y_added")

        newton = ["guess"] + [f"{q}{i}" for i in range(NEWTON) for q in ("yy", "vyy", "half", "y")]
        f_pe = [Marks(sem(f"ffn{i}_pe"), "T0 T1 k0 k1 r0 r1 v0 v1") for i in range(2)]
        f_act = [Marks(sem(f"ffn{i}_act"), "ln0 ln1 xn0 xn1 lead last pk0 pk1 pk2 pk3 "
                       "pr0 pr1 pr2 pr3 rel0 sq0 rel1 sq1 th0 th1") for i in range(2)]
        f_dve = [Marks(sem(f"ffn{i}_dve"), "st0 st1 mv0 mv1 xk0 xk1 xk2 xk3 xr0 xr1 xr2 xr3 g0 g1"
                       + " o0 o1" * (i == 0)) for i in range(2)]
        f_pool = [Marks(sem(f"ffn{i}_pool"), ["v"] + newton + ["mean", "shift"] + ["o"] * (i == 1))
                  for i in range(2)]
        m_pe = Marks(sem("mamba_pe"), "T0 T1 xs0 xs1 xs2 xs3 xp")
        m_act = Marks(sem("mamba_act"), "xn0 xn1 xn2 xn3 raw0 lead0 last0 tapa0 tapb0 "
                      "raw1 lead1 last1 tapa1 tapb1 th0 th1 raw2 lead2 last2 tapa2 tapb2 "
                      "raw3 lead3 last3 tapa3 tapb3 th2 th3 xp")
        taps = [f"c{q}{c}" for q in range(KC - 1) for c in "ab"]
        m_dve = Marks(sem("mamba_dve"), ["st0", "st1", "mv0", "mv1", "in0", "in1", "ln0", "ln1"] + [
            t for do in "t0 t1 s0 s1 t2 t3 s2 s3".split()
            for t in ([q + do[1] for q in taps] if do[0] == "t" else ["silu" + do[1]])])
        m_pool = Marks(sem("mamba_pool"), ["v", "v2"] + newton + ["res"])
        h_pe = Marks(sem("half_pe"), "dt0_0 dt0_1 C sd0_0 sd0_1 dt1_0 dt1_1 sd1_0 sd1_1")
        h_act = Marks(sem("half_act"), "xa0 xb0 xc0 xd0 abs0 exp0 ln0 da0 db0 dc0 dd0 C ya0 yb0 "
                      "xa1 xb1 xc1 xd1 abs1 exp1 ln1 da1 db1 dc1 dd1 ya1 yb1")
        h_dve = Marks(sem("half_dve"), "delta0 delta1")
        h_pool = Marks(sem("half_pool"), "u0 u1")
        z_pe = Marks(sem("gate_pe"), "0 1 2 3")
        z_act = Marks(sem("gate_act"), "0 1 2 3")
        z_dve = Marks(sem("gate_dve"), "0 1 2 3")
        y_pe = Marks(sem("y_pe"), "T0 T1 T2 T3 o0 half1 o1")
        y_dve = Marks(sem("y_dve"), "g0 g1 g2 g3 x0 x1")

        GROUPS = [("f0T0", 1, f_act[0], "xn0"), ("f0T1", 1, f_act[0], "xn1"),
                  ("z0", 0, z_dve, "0"), ("YT2", -1, y_dve, "g2"), ("YT3", -1, y_dve, "g3"),
                  ("f0k0", 1, f_act[0], "rel0"), ("f0k1", 1, f_act[0], "rel1"),
                  ("f0r0", 1, f_act[0], "th0"), ("f0r1", 1, f_act[0], "th1"),
                  ("f0v0", 1, f_dve[0], "g0"), ("dt1_0", 0, h_act, "xb1"),
                  ("f0v1", 1, f_dve[0], "g1"), ("dt1_1", 0, h_act, "xd1"), ("o0", -1, y_dve, "x0"),
                  ("o1", -1, y_dve, "x1"), ("mT0", 1, m_act, "xn1"), ("mT1", 1, m_act, "xn3"),
                  ("z1", 0, z_dve, "1"), ("xs0", 1, m_act, "tapb0"), ("sd1_0", 0, h_act, "ya1"),
                  ("sd1_1", 0, h_act, "yb1"), ("xs1", 1, m_act, "tapb1"),
                  ("f1T0", -1, f_act[1], "xn0"), ("f1T1", -1, f_act[1], "xn1"),
                  ("xs2", 1, m_act, "tapb2"), ("z2", 0, z_dve, "2"), ("xs3", 1, m_act, "tapb3"),
                  ("f1k0", -1, f_act[1], "rel0"), ("f1k1", -1, f_act[1], "rel1"),
                  ("xp", 1, m_act, "xp"), ("f1r0", -1, f_act[1], "th0"),
                  ("dt0_0", 1, h_act, "xb0"), ("dt0_1", 1, h_act, "xd0"),
                  ("f1r1", -1, f_act[1], "th1"), ("f1v0", -1, f_dve[1], "g0"),
                  ("f1v1", -1, f_dve[1], "g1"), ("C", 1, h_act, "C"), ("YT0", 0, y_dve, "g0"),
                  ("YT1", 0, y_dve, "g1"), ("z3", 0, z_dve, "3"), ("sd0_0", 1, h_act, "ya0"),
                  ("sd0_1", 1, h_act, "yb0")]
        SLOTS = -(-len(GROUPS) // BANKS) * BANKS
        NUMBER = {g[0]: n for n, g in enumerate(GROUPS)}

        def bank(group):
            return mm[:, NUMBER[group] % BANKS, :]

        def bank_free(it, group):
            n = NUMBER[group] - BANKS
            while True:
                if n < 0:
                    n, it = n + SLOTS, it - 1
                if n < len(GROUPS):
                    _, off, marks, name = GROUPS[n]
                    if not isinstance(it, int) or 0 <= it + off < NCH:
                        return marks.sem, marks.at(it + off, name)
                if it < -2:
                    return None
                n -= BANKS

        def soft(hf):
            return u[:, 0, :, :].rearrange("p e w -> p (e w)") if hf == 0 else \
                ffn_row[1][:, :, :].rearrange("p b d -> p (b d)")

        def mix(i, q):
            return ffn_mix[i if q == 1 else 1 - i]

        def col3(t):
            return t.rearrange("p (b t) -> p b t", b=B)

        def fcol(i, ct, lo):
            return ffn_col[i][:, ct, :].rearrange("p (b s) -> p b s", b=B)[:, :, lo:lo + T]

        def run(body, eng):
            for it in (-2, -1, 0, 1):
                body(it, it % PAIRS)
            with eng.Fori(1, NCH // PAIRS - 1) as turn:
                for pair in range(PAIRS):
                    body(turn * PAIRS + pair, pair)
            for it in (NCH - 2, NCH - 1, NCH, NCH + 1):
                body(it, it % PAIRS)

        def has(it, off):
            return not isinstance(it, int) or 0 <= it + off < NCH

        block = ctx.enter_context(nc.Block())

        @block.sync
        def _(sp):
            def rows_of(dram, k, pair, tb):
                return dram[B * pair + tb, bass.ds((k - pair) * (T // PAIRS), T), :]

            def load_x(k, pair):
                if due(count := m_pool.at(k - 1, "res")):
                    sp.wait_ge(m_pool.sem, count)
                    sp.sem_inc(passed_sp, 1)
                if due(count := m_dve.at(k - 1, "ln1")):
                    sp.wait_ge(m_dve.sem, count)
                    sp.sem_inc(passed_sp, 1)
                for tb in range(TB):
                    sp.dma_start(xin[:, tb, :], rows_of(x, k, pair, tb)).then_inc(x_loaded, 16)

            for i, v in ((0, mu_r), (1, mu_k), (4, ln_w), (5, ln_b)):
                sp.dma_start(vec[:, i, :], v).then_inc(v_loaded, 16)
            for i, v in ((0, b_conv), (1, b_dt), (2, d_skip)):
                sp.dma_start(evec[:, i, :], v).then_inc(v_loaded, 16)
            sp.dma_start(conv_sb[:, :, :], w_conv.rearrange("(t p) k -> p t k", p=P)).then_inc(v_loaded, 16)
            sp.dma_start(neg_a[:, :, :], a_log.rearrange("(t p) n -> p t n", p=P)).then_inc(v_loaded, 16)
            load_x(0, 0)
            for dst, src, loaded in ((wk_sb, w_k, wk_loaded), (wr_sb, w_r, wr_loaded),
                                     (wv_sb, w_v, wv_loaded), (win_sb, w_in, win_loaded),
                                     (wx_sb, w_x, wx_loaded)):
                sp.dma_start(dst[:, :, :], src.rearrange("(t p) n -> p t n", p=P)).then_inc(loaded, 16)
            sp.wait_ge(init_pool, 2)
            sp.dma_start(wdt_sb[0:R, :], w_dt).then_inc(wdt_loaded, 16)
            sp.dma_start(wout_sb[:, :, :], w_out.rearrange("(t p) n -> p t n", p=P)).then_inc(wout_loaded, 16)

            def load_b(k, j):
                if j < 2:
                    if due(count := 16 * (k + 1)):
                        sp.wait_ge(b_stored, count)
                        sp.sem_inc(passed_sp, 1)
                if due(count := 2 * NSTEP * k + 2 * NBG * (j - 1)):
                    sp.wait_ge(dbx_done, count)
                    sp.sem_inc(passed_sp, 1)
                sp.dma_start(b_all[:, j % 2, :, :],
                             b_dram[bass.ds(k, 1), j % (NS // NBG) * NBG * W:(j % (NS // NBG) + 1) * NBG * W]
                             .rearrange("o (n w) -> o n w", n=NBG).broadcast_to([P, NBG, W])
                             ).then_inc(b_loaded[j % 2], 16)

            def body(it, pair):
                if has(it, -2):
                    sp.wait_ge(f_pool[1].sem, f_pool[1].at(it - 2, "o"))
                    sp.sem_inc(passed_sp, 1)
                    for tb in range(TB):
                        sp.dma_start(rows_of(out, it - 2, pair, tb), xout[:, tb, :]).then_inc(out_stored, 16)
                if has(it, 0):
                    for j in range(2, 11):
                        load_b(it, j)
                if has(it, 2) and has(it, 1):
                    load_x(it + 2, pair)
                if has(it, 0):
                    for j in range(11, NG):
                        load_b(it, j)
                if has(it, 1):
                    sp.wait_ge(m_act.sem, m_act.at(it + 1, "xp"))
                    sp.sem_inc(passed_sp, 1)
                    sp.dma_start(b_dram[bass.ds(it + 1, 1), :].rearrange("o (n w) -> (o n) w", n=NS),
                                 xdbl[R:R + NS, :]).then_inc(b_stored, 16)
                    load_b(it + 1, 0)
                    load_b(it + 1, 1)
            run(body, sp)
            sp.wait_ge(out_stored, 16 * TB * NCH)

        @block.tensor
        def _(pe):
            pe.wait_ge(init_pool, 3)

            def first(it):
                return isinstance(it, int) and it < 2

            def turn_rows(it, group, src, marks):
                for j in range(2):
                    if free := bank_free(it, group + f"T{j}"):
                        pe.wait_ge(*free)
                    o = bank(group + f"T{j}").rearrange("p (c w) -> p c w", c=2)
                    for c in range(2):
                        for tb in range(TB):
                            ct = 2 * j + c
                            last = pe.transpose(o[:, c, tb * P:(tb + 1) * P],
                                                src[:, tb, ct * P:(ct + 1) * P], ident[:, :])
                    last.then_inc(marks.sem, 1)

            def ffn_turn(it, i, k):
                pe.wait_ge(f_act[i].sem, f_act[i].at(k, "ln1"))
                turn_rows(it, f"f{i}", ffn_row[i], f_pe[i])

            def ffn_r(it, i, k, tb):
                pe.wait_ge(f_dve[i].sem, f_dve[i].at(k, "xr3"))
                if free := bank_free(it, f"f{i}r{tb}"):
                    pe.wait_ge(*free)
                if first(it):
                    pe.wait_ge(wr_loaded, 16)
                for ct in range(CT):
                    last = pe.matmul(bank(f"f{i}r{tb}"), mix(i, 0)[:, ct, tb * P:(tb + 1) * P],
                                     wr_sb[:, ct, :], start=ct == 0, stop=ct == CT - 1)
                last.then_inc(f_pe[i].sem, 1)

            def ffn_k(it, i, k, j):
                pe.wait_ge(f_dve[i].sem, f_dve[i].at(k, "xk3"))
                if free := bank_free(it, f"f{i}k{j}"):
                    pe.wait_ge(*free)
                if first(it):
                    pe.wait_ge(wk_loaded, 16)
                o = bank(f"f{i}k{j}").rearrange("p (c w) -> p c w", c=2)
                for c in range(2):
                    dt = 2 * j + c
                    for ct in range(CT):
                        last = pe.matmul(o[:, c, :], wk_sb[:, ct, dt * P:(dt + 1) * P],
                                         mix(i, 1)[:, ct, :], start=ct == 0, stop=ct == CT - 1)
                last.then_inc(f_pe[i].sem, 1)

            def ffn_v(it, i, k, tb):
                pe.wait_ge(f_act[i].sem, f_act[i].at(k, "sq1"))
                if free := bank_free(it, f"f{i}v{tb}"):
                    pe.wait_ge(*free)
                if first(it):
                    pe.wait_ge(wv_loaded, 16)
                for ct in range(CT):
                    last = pe.matmul(bank(f"f{i}v{tb}"), ffn_col[i][:, ct, tb * P:(tb + 1) * P],
                                     wv_sb[:, ct, :], start=ct == 0, stop=ct == CT - 1)
                last.then_inc(f_pe[i].sem, 1)

            def mamba_turn(it, k):
                pe.wait_ge(m_dve.sem, m_dve.at(k, "in1"))
                turn_rows(it, "m", ffn_row[0], m_pe)

            def project(it, group, e0, marks, pair):
                if free := bank_free(it, group):
                    pe.wait_ge(*free)
                if first(it):
                    pe.wait_ge(win_loaded, 16)
                o = bank(group).rearrange("p (c w) -> p c w", c=2)
                for c in range(2):
                    for ct in range(CT):
                        last = pe.matmul(o[:, c, :], win_sb[:, ct, e0 + c * P:e0 + (c + 1) * P],
                                         xn_col[:, pair, ct, :], start=ct == 0, stop=ct == CT - 1)
                last.then_inc(marks.sem, 1)

            def xs(it, k, j, pair):
                pe.wait_ge(m_act.sem, m_act.at(k, "xn3"))
                project(it, f"xs{j}", 2 * j * P, m_pe, pair)

            def z(it, j, pair):
                project(it, f"z{j}", E + 2 * j * P, z_pe, pair)

            def xproj(it, k, part):
                pe.wait_ge(m_dve.sem, m_dve.at(k, f"silu{2 * part + 1}"))
                if part == 0:
                    if free := bank_free(it, "xp"):
                        pe.wait_ge(*free)
                if first(it):
                    pe.wait_ge(wx_loaded, 16)
                for et in range(HT * part, HT * part + HT):
                    last = pe.matmul(bank("xp")[0:XR, 0:W], wx_sb[:, et, :], xc2[:, et, :],
                                     start=et == 0, stop=et == ET - 1)
                if part == 1:
                    last.then_inc(m_pe.sem, 1)

            def turn_c(it, k):
                pe.wait_ge(m_act.sem, m_act.at(k, "xp"))
                if free := bank_free(it, "C"):
                    pe.wait_ge(*free)
                for tb in range(TB):
                    last = pe.transpose(bank("C")[:, tb * P:(tb + 1) * P],
                                        xdbl[:, tb * P:(tb + 1) * P], ident[:, :])
                last.then_inc(h_pe.sem, 1)

            def dt_proj(it, k, hf, j):
                pe.wait_ge(m_act.sem, m_act.at(k, "xp"))
                if free := bank_free(it, f"dt{hf}_{j}"):
                    pe.wait_ge(*free)
                if first(it):
                    pe.wait_ge(wdt_loaded, 16)
                o = bank(f"dt{hf}_{j}").rearrange("p (c w) -> p c w", c=2)
                for c in range(2):
                    et = HT * hf + 2 * j + c
                    last = pe.matmul(o[:, c, :], wdt_sb[:, et * P:(et + 1) * P], xdbl[:, :],
                                     start=True, stop=True)
                last.then_inc(h_pe.sem, 1)

            def turn_skip(it, k, hf, tb):
                pe.wait_ge(h_act.sem, h_act.at(k, f"dd{hf}"))
                if free := bank_free(it, f"sd{hf}_{tb}"):
                    pe.wait_ge(*free)
                for e in range(HT):
                    last = pe.transpose(bank(f"sd{hf}_{tb}")[:, e * P:(e + 1) * P],
                                        ffn_mix[1][:, e, tb * P:(tb + 1) * P], ident[:, :])
                last.then_inc(h_pe.sem, 1)

            def turn_y(it, k, j):
                hf = j // 2
                if due(count := NSTT * k + TB * NS * (hf + 1)):
                    pe.wait_ge(y_added, count)
                if free := bank_free(it, f"YT{j}"):
                    pe.wait_ge(*free)
                o = bank(f"YT{j}").rearrange("p (c w) -> p c w", c=2)
                for c in range(2):
                    e = 2 * (j % 2) + c
                    for tb in range(TB):
                        last = pe.transpose(o[:, c, tb * P:(tb + 1) * P],
                                            y_rows[:, hf, tb, e * P:(e + 1) * P], ident[:, :])
                last.then_inc(y_pe.sem, 1)

            def out_proj(it, k, tb, part):
                if part == 0:
                    pe.wait_ge(y_dve.sem, y_dve.at(k, "g3"))
                    if free := bank_free(it, f"o{tb}"):
                        pe.wait_ge(*free)
                if first(it):
                    pe.wait_ge(wout_loaded, 16)
                gated, half = ((u[:, 1, :, :], 1), (ffn_col[1], 0))[part]
                for e in range(HT):
                    last = pe.matmul(bank(f"o{tb}"), gated[:, e, tb * P:(tb + 1) * P],
                                     wout_sb[:, HT * half + e, :], start=part == 0 and e == 0,
                                     stop=part == 1 and e == HT - 1)
                if part == 1 or tb == 1:
                    last.then_inc(y_pe.sem, 1)

            def turn_h(it, s, tb):
                if tb == 0:
                    if due(count := NSTEP * it + s + 1):
                        pe.wait_ge(scan_done, count)
                if due(count := NSTT * it + TB * (s - 2) + tb + 1):
                    pe.wait_ge(y_added, count)
                for e in range(HT):
                    last = pe.transpose(h_rows[:, s % 2, tb, e * P:(e + 1) * P],
                                        h[:, s % RING, e, tb, 1:SEG], ident[:, :])
                last.then_inc(h_turned, 1)

            def body(it, pair):
                scan, front, back = has(it, 0), has(it, 1), has(it, -1)
                f, b = it + 1, it - 1
                for s in range(NSTEP):
                    if scan:
                        turn_h(it, s, 0)
                        turn_h(it, s, 1)
                    if front and s == 0:
                        ffn_turn(it, 0, f)
                    if scan and s == 0:
                        z(it, 0, pair)
                    if back and s == 2:
                        turn_y(it, b, 2)
                        turn_y(it, b, 3)
                    if front:
                        if s in (2, 3):
                            ffn_k(it, 0, f, s - 2)
                        if s in (4, 5):
                            ffn_r(it, 0, f, s - 4)
                    if scan and s in (7, 8):
                        dt_proj(it, it, 1, s - 7)
                    if front and s in (6, 7):
                        ffn_v(it, 0, f, s - 6)
                    if back and 8 <= s < 12:
                        out_proj(it, b, (s - 8) // 2, s % 2)
                    if front and s == 12:
                        mamba_turn(it, f)
                    if scan and s == 12:
                        z(it, 1, pair)
                    if front and s in (14, 15):
                        xs(it, f, s - 14, 1 - pair)
                    if scan and s == 14:
                        turn_skip(it, it, 1, 0)
                        turn_skip(it, it, 1, 1)
                    if back and s == 15:
                        ffn_turn(it, 1, b)
                    if front and s in (17, 19):
                        xs(it, f, (s - 13) // 2, 1 - pair)
                    if scan and s == 18:
                        z(it, 2, pair)
                    if back and s in (20, 21):
                        ffn_k(it, 1, b, s - 20)
                    if front:
                        if s in (22, 23):
                            xproj(it, f, s - 22)
                    if back and s == 23:
                        ffn_r(it, 1, b, 0)
                    if front and s == 24:
                        dt_proj(it, f, 0, 0)
                        dt_proj(it, f, 0, 1)
                    if back:
                        if s == 26:
                            ffn_r(it, 1, b, 1)
                        if s in (27, 28):
                            ffn_v(it, 1, b, s - 27)
                    if front and s == 28:
                        turn_c(it, f)
                    if scan and s == 30:
                        turn_y(it, it, 0)
                        turn_y(it, it, 1)
                        z(it, 3, pair)
                    if front and s == 31:
                        turn_skip(it, f, 0, 0)
                        turn_skip(it, f, 0, 1)

            run(body, pe)

        @block.scalar
        def _(act):
            act.wait_ge(v_loaded, 16 * 9)
            act.activation(neg_a[:, :, :], neg_a[:, :, :], ACT.Exp).then_inc(init_act, 1)
            act.wait_ge(init_act, 1)
            act.activation(neg_a[:, :, :], neg_a[:, :, :], ACT.Copy, scale=-1.0).then_inc(init_act, 1)
            act.wait_ge(init_act, 2)
            act.wait_ge(init_dve, 3)
            act.wait_ge(init_pool, 11)

            def ffn_norm(i, k, scanned=True):
                act.wait_ge(f_pool[i].sem, f_pool[i].at(k, "shift"))
                if i == 0:
                    if due(count := m_pe.at(k - 1, "T1")):
                        act.wait_ge(m_pe.sem, count)
                    if due(count := m_dve.at(k - 1, "silu3")):
                        act.wait_ge(m_dve.sem, count)
                else:
                    if due(count := f_pool[1].at(k - 1, "o")):
                        act.wait_ge(f_pool[1].sem, count)
                    act.wait_ge(h_dve.sem, h_dve.at(k + 1 if scanned else k, "delta1"))
                for tb in range(TB):
                    act.activation(ffn_row[i][:, tb, :], (xin, xout)[i][:, tb, :], ACT.Identity,
                                   scale=rs[i][:, tb:tb + 1],
                                   bias=shift[i][:, tb:tb + 1]).then_inc(f_act[i].sem, 1)

            def ffn_columns(i, k, pair):
                if i == 1:
                    act.wait_ge(y_pe.sem, y_pe.at(k, "o1"))
                if due(count := f_pe[i].at(k - 1, "v1")):
                    act.wait_ge(f_pe[i].sem, count)
                for j in range(2):
                    act.wait_ge(f_pe[i].sem, f_pe[i].at(k, f"T{j}"))
                    for_j = ffn_col[i][:, 2 * j:2 * j + 2, :].rearrange("p c (b s) -> p (c b) s", b=B)
                    act.activation(for_j[:, :, 1:SEG],
                                   bank(f"f{i}T{j}").rearrange("p (q t) -> p q t", t=T),
                                   ACT.Copy).then_inc(f_act[i].sem, 1)
                both = ffn_col[i][:, :, :].rearrange("p c (b s) -> p (c b) s", b=B)
                last = ffn_last[i][:, pair, :, :].rearrange("p c b -> p (c b)").unsqueeze(2)
                if due(count := f_act[i].at(k - 1, "last")):
                    act.wait_ge(f_act[i].sem, count)
                act.activation(both[:, :, 0:1], last, ACT.Copy).then_inc(f_act[i].sem, 1)
                act.wait_ge(f_act[i].sem, f_act[i].at(k, "lead"))
                act.activation(last, both[:, :, T:SEG], ACT.Copy).then_inc(f_act[i].sem, 1)

            def ffn_before(i, k, q, scanned=True, fronted=True):
                act.wait_ge(f_act[i].sem, f_act[i].at(k, "lead"))
                if i == 0:
                    if q == 1:
                        if due(count := f_pe[0].at(k - 1, "k1")):
                            act.wait_ge(f_pe[0].sem, count)
                        if due(count := f_pe[1].at(k - 3, "r1")):
                            act.wait_ge(f_pe[1].sem, count)
                    else:
                        if due(count := h_pe.at(k - 1, "sd0_1")):
                            act.wait_ge(h_pe.sem, count)
                elif q == 1:
                    act.wait_ge(h_pe.sem, h_pe.at(k + 1 if scanned else k, "sd1_1"))
                    if due(count := f_pe[1].at(k - 1, "k1")):
                        act.wait_ge(f_pe[1].sem, count)
                else:
                    if fronted:
                        act.wait_ge(f_pe[0].sem, f_pe[0].at(k + 2, "k1"))
                    if due(count := f_pe[1].at(k - 1, "r1")):
                        act.wait_ge(f_pe[1].sem, count)
                for ct in range(CT):
                    act.activation(col3(mix(i, q)[:, ct, :]), fcol(i, ct, 0), ACT.Copy,
                                   scale=vec[:, 2 + q, ct:ct + 1]).then_inc(f_act[i].sem, 1)

            def ffn_tanh(i, k, tb):
                act.wait_ge(f_pe[i].sem, f_pe[i].at(k, f"r{tb}"))
                act.activation(ffn_row[i][:, tb, :], bank(f"f{i}r{tb}"), ACT.Tanh,
                               scale=0.5).then_inc(f_act[i].sem, 1)

            def ffn_relu2(i, k, j):
                act.wait_ge(f_pe[i].sem, f_pe[i].at(k, f"k{j}"))
                act.wait_ge(f_dve[i].sem, f_dve[i].at(k, "xr3"))
                o = ffn_col[i][:, 2 * j:2 * j + 2, 0:W]
                act.activation(o, bank(f"f{i}k{j}").rearrange("p (c w) -> p c w", c=2),
                               ACT.Relu).then_inc(f_act[i].sem, 1)
                act.wait_ge(f_act[i].sem, f_act[i].at(k, f"rel{j}"))
                act.activation(o, o, ACT.Square, scale=0.5).then_inc(f_act[i].sem, 1)

            def mamba_columns(k, pair):
                if due(count := z_pe.at(k - 2, "3")):
                    act.wait_ge(z_pe.sem, count)
                for ct in range(CT):
                    if ct % 2 == 0:
                        act.wait_ge(m_pe.sem, m_pe.at(k, f"T{ct // 2}"))
                    act.activation(xn_col[:, pair, ct, :], bank(f"mT{ct // 2}")[:, (ct % 2) * W:(ct % 2 + 1) * W],
                                   ACT.Identity, scale=vec[:, 4, ct:ct + 1],
                                   bias=vec[:, 5, ct:ct + 1]).then_inc(m_act.sem, 1)

            def conv_start(k, j, pair):
                act.wait_ge(m_pe.sem, m_pe.at(k, f"xs{j}"))
                if j >= 2:
                    act.wait_ge(m_dve.sem, m_dve.at(k, f"c2b{j - 2}"))
                else:
                    if due(count := m_dve.at(k - 1, f"c2b{j + 2}")):
                        act.wait_ge(m_dve.sem, count)
                pad = xs_pad[:, j % 2, :, :, :].rearrange("p c b s -> p (c b) s")
                hist = xs_last[:, pair, 2 * j:2 * j + 2, :, :].rearrange("p c b s -> p (c b) s")
                src = bank(f"xs{j}")
                act.activation(pad[:, :, KC - 1:], src.rearrange("p (q t) -> p q t", t=T),
                               ACT.Copy).then_inc(m_act.sem, 1)
                if due(count := m_act.at(k - 1, f"last{j}")):
                    act.wait_ge(m_act.sem, count)
                act.activation(pad[:, :, 0:KC - 1], hist, ACT.Copy).then_inc(m_act.sem, 1)
                act.wait_ge(m_act.sem, m_act.at(k, f"lead{j}"))
                act.activation(hist, pad[:, :, T:T + KC - 1], ACT.Copy).then_inc(m_act.sem, 1)
                if due(count := h_pool.at(k - 1, "u1")):
                    act.wait_ge(h_pool.sem, count)
                if due(count := h_act.at(k - 1, "dd1")):
                    act.wait_ge(h_act.sem, count)
                for c in range(2):
                    et = 2 * j + c
                    act.activation(xc2[:, et, :], src[:, c * W:(c + 1) * W], ACT.Identity,
                                   scale=conv_sb[:, et, KC - 1:KC],
                                   bias=evec[:, 0, et:et + 1]).then_inc(m_act.sem, 1)

            def conv_tanh(k, j):
                act.wait_ge(m_dve.sem, m_dve.at(k, f"c2b{j}"))
                if j >= 2:
                    act.wait_ge(m_dve.sem, m_dve.at(k, f"silu{j - 2}"))
                elif due(count := m_dve.at(k - 1, f"silu{j + 2}")):
                    act.wait_ge(m_dve.sem, count)
                act.activation(ffn_row[0][:, j % 2, :], xc2[:, 2 * j:2 * j + 2, :].rearrange("p c w -> p (c w)"),
                               ACT.Tanh, scale=0.5).then_inc(m_act.sem, 1)

            def x_rows(k):
                act.wait_ge(m_pe.sem, m_pe.at(k, "xp"))
                if due(count := h_pe.at(k - 1, "dt1_1")):
                    act.wait_ge(h_pe.sem, count)
                if due(count := 16 * k):
                    act.wait_ge(b_stored, count)
                act.activation(xdbl[0:XR, :], bank("xp")[0:XR, 0:W], ACT.Copy,
                               scale=xscale[:, 0:1]).then_inc(m_act.sem, 1)

            def keep_c(k, pair):
                act.wait_ge(h_pe.sem, h_pe.at(k, "C"))
                if due(count := NSTT * (k - 1)):
                    act.wait_ge(y_added, count)
                act.activation(c_rows[:, pair, :, :],
                               bank("C").rearrange("p (q c) -> p q c", c=P)[:, 0:TB, R + NS:XR],
                               ACT.Copy).then_inc(h_act.sem, 1)

            def softplus_x(k, hf, j):
                if j == 0:
                    if due(count := NEXP * (k - 1) + NEXP // 2 * (hf + 1)):
                        act.wait_ge(decay_done, count)
                act.wait_ge(h_pe.sem, h_pe.at(k, f"dt{hf}_{j}"))
                for e in (2 * j, 2 * j + 1):
                    act.activation(delta[:, hf, e, :], bank(f"dt{hf}_{j}")[:, (e % 2) * W:(e % 2 + 1) * W],
                                   ACT.Identity,
                                   bias=evec[:, 1, HT * hf + e:HT * hf + e + 1]).then_inc(h_act.sem, 1)

            def softplus_exp(k, hf):
                if hf == 0:
                    if due(count := 2 * NSTEP * (k - 1) + NSTEP):
                        act.wait_ge(dbx_done, count)
                else:
                    if due(count := f_pool[1].at(k - 2, "o")):
                        act.wait_ge(f_pool[1].sem, count)
                    if due(count := h_dve.at(k - 1, "delta1")):
                        act.wait_ge(h_dve.sem, count)
                act.wait_ge(h_act.sem, h_act.at(k, f"xd{hf}"))
                act.activation(soft(hf), delta[:, hf, :, :].rearrange("p e w -> p (e w)"),
                               ACT.Abs).then_inc(h_act.sem, 1)
                act.wait_ge(h_act.sem, h_act.at(k, f"abs{hf}"))
                act.activation(soft(hf), soft(hf), ACT.Exp, scale=-1.0).then_inc(h_act.sem, 1)

            def softplus_ln(k, hf):
                act.wait_ge(h_act.sem, h_act.at(k, f"exp{hf}"))
                act.activation(soft(hf), soft(hf), ACT.Ln, bias=1.0).then_inc(h_act.sem, 1)

            def skip_columns(k, hf, fronted=True):
                if hf == 0:
                    act.wait_ge(f_pe[0].sem, f_pe[0].at(k, "r1"))
                    if due(count := f_pe[1].at(k - 2, "k1")):
                        act.wait_ge(f_pe[1].sem, count)
                    if due(count := h_pe.at(k - 1, "sd1_1")):
                        act.wait_ge(h_pe.sem, count)
                else:
                    if fronted:
                        act.wait_ge(f_pe[0].sem, f_pe[0].at(k + 1, "r1"))
                    act.wait_ge(h_pe.sem, h_pe.at(k, "sd0_1"))
                for e in range(HT):
                    et = HT * hf + e
                    act.activation(ffn_mix[1][:, e, :], xc2[:, et, :], ACT.Copy,
                                   scale=evec[:, 3, et:et + 1]).then_inc(h_act.sem, 1)

            def skip_rows(k, hf, tb):
                act.wait_ge(h_pe.sem, h_pe.at(k, f"sd{hf}_{tb}"))
                if due(count := y_pe.at(k - 1, f"T{2 * hf + 1}")):
                    act.wait_ge(y_pe.sem, count)
                act.activation(y_rows[:, hf, tb, :], bank(f"sd{hf}_{tb}"), ACT.Copy).then_inc(h_act.sem, 1)

            def gate_tanh(k, j):
                act.wait_ge(z_pe.sem, z_pe.at(k, f"{j}"))
                if due(count := y_dve.at(k - 1, f"g{j}")):
                    act.wait_ge(y_dve.sem, count)
                act.activation(gate[:, 2 * j:2 * j + 2, :].rearrange("p c w -> p (c w)"), bank(f"z{j}"),
                               ACT.Tanh, scale=0.5).then_inc(z_act.sem, 1)

            def decays(it, s):
                hf, n = divmod(s, NS)
                act.wait_ge(h_dve.sem, h_dve.at(it, f"delta{hf}"))
                if due(count := NSTEP * it + s - 1):
                    act.wait_ge(scan_done, count)
                for e in range(HT):
                    act.activation(decay[:, s % 2, e, :, 1:SEG], col3(delta[:, hf, e, :]), ACT.Exp,
                                   scale=neg_a[:, HT * hf + e, n:n + 1]).then_inc(decay_done, 1)

            def save(it, s, pair):
                if due(count := NSTEP * it + s + 1):
                    act.wait_ge(scan_done, count)
                if due(count := 2 * NSTEP * it + 2 * s + 1):
                    act.wait_ge(dbx_done, count)
                act.activation(state[:, pair, s, :, :], h[:, s % RING, :, :, T], ACT.Copy).then_inc(saved, 1)

            def body(it, pair):
                scan, front, back, ahead = has(it, 0), has(it, 1), has(it, -1), has(it, 2)
                f, b = it + 1, it - 1
                other = (pair + 1) % PAIRS
                for s in range(NSTEP):
                    if scan:
                        decays(it, s)
                    if s < SAVE:
                        if back:
                            save(b, NSTEP - SAVE + s, other)
                    elif scan:
                        save(it, s - SAVE, pair)
                    if back and s == 2:
                        gate_tanh(b, 3)
                    if scan and s == 2:
                        skip_rows(it, 0, 0)
                        skip_rows(it, 0, 1)
                    if front:
                        if s == 2:
                            ffn_columns(0, f, other)
                            ffn_before(0, f, 1)
                        if s == 4:
                            ffn_before(0, f, 0)
                    if scan and s == 4:
                        gate_tanh(it, 0)
                    if front:
                        if s in (4, 5):
                            ffn_relu2(0, f, s - 4)
                        if s in (10, 11):
                            ffn_tanh(0, f, s - 10)
                    if scan:
                        if s == 10:
                            softplus_x(it, 1, 0)
                        if s == 11:
                            softplus_x(it, 1, 1)
                            softplus_exp(it, 1)
                        if s == 11:
                            softplus_ln(it, 1)
                        if s == 13:
                            skip_columns(it, 1, front)
                    if front:
                        if s == 16:
                            mamba_columns(f, other)
                        if s == 17:
                            conv_start(f, 0, other)
                    if scan and s == 16:
                        gate_tanh(it, 1)
                    if back and s == 18:
                        ffn_norm(1, b, scan)
                    if scan and s == 18:
                        skip_rows(it, 1, 0)
                        skip_rows(it, 1, 1)
                    if front and s == 18:
                        conv_start(f, 1, other)
                    if back and s == 18:
                        ffn_columns(1, b, other)
                    if front and s in (19, 20):
                        conv_tanh(f, s - 19)
                    if back and s == 19:
                        ffn_before(1, b, 1, scan, front)
                    if scan and s == 21:
                        gate_tanh(it, 2)
                    if front and s in (21, 22):
                        conv_start(f, s - 19, other)
                    if back and s == 21:
                        ffn_before(1, b, 0, scan, front)
                    if front and s in (22, 23):
                        conv_tanh(f, s - 20)
                    if back and s in (25, 26):
                        ffn_relu2(1, b, s - 25)
                    if front:
                        if s == 27:
                            x_rows(f)
                    if back and s == 27:
                        ffn_tanh(1, b, 0)
                    if front:
                        if s == 28:
                            softplus_x(f, 0, 0)
                            softplus_x(f, 0, 1)
                        if s == 29:
                            softplus_exp(f, 0)
                    if ahead and s == 28:
                        ffn_norm(0, it + 2)
                    if back and s == 31:
                        ffn_tanh(1, b, 1)
                    if front:
                        if s == 30:
                            softplus_ln(f, 0)
                        if s == 31:
                            skip_columns(f, 0)
                            keep_c(f, other)
            run(body, act)

        @block.vector
        def _(dve):
            dve.memset(decay[:, :, :, :, :], 0.0).then_inc(init_dve, 1)
            dve.wait_ge(v_loaded, 16 * 9)
            dve.tensor_scalar(vec[:, 2:4, :], vec[:, 0:2, :], -1.0, 1.0, ALU.mult,
                              ALU.add).then_inc(init_dve, 1)
            dve.tensor_scalar(evec[:, 3, :], evec[:, 2, :], 0.5, None, ALU.mult).then_inc(init_dve, 1)
            dve.wait_ge(init_dve, 3)

            def norm_stats(q, marks, k, src):
                for tb in range(TB):
                    dve.bn_stats(stats[q][:, tb, :], src[:, tb, :]).then_inc(marks.sem, 1)
                for tb in range(TB):
                    dve.wait_ge(marks.sem, marks.at(k, f"st{tb}"))
                    dve.sem_inc(passed_dve, 1)
                    dve.bn_aggr(mv[q][:, tb, :], stats[q][:, tb, :]).then_inc(marks.sem, 1)

            def normalise(q, pool_marks, marks, k, src, dst, r0):
                dve.wait_ge(pool_marks.sem, pool_marks.at(k, f"y{NEWTON - 1}"))
                for tb in range(TB):
                    dve.tensor_scalar(dst[:, tb, :], src[:, tb, :], mv[q][:, tb, 0:1],
                                      rs[q][:, r0 + tb:r0 + tb + 1], ALU.subtract,
                                      ALU.mult).then_inc(marks.sem, 1)

            def ffn_stats(i, k, src):
                if due(count := f_pool[i].at(k - 1, "mean")):
                    dve.wait_ge(f_pool[i].sem, count)
                norm_stats(i, f_dve[i], k, src)

            def ffn_mix_in(i, k, q):
                for ct in range(CT):
                    dve.wait_ge(f_act[i].sem, f_act[i].at(k, f"{'pr' if q == 0 else 'pk'}{ct}"))
                    m = col3(mix(i, q)[:, ct, :])
                    dve.scalar_tensor_tensor(out=m, in0=fcol(i, ct, 1), scalar=vec[:, q, ct:ct + 1],
                                             in1=m, op0=ALU.mult, op1=ALU.add).then_inc(f_dve[i].sem, 1)

            def ffn_gate(i, k, tb):
                dve.wait_ge(f_pe[i].sem, f_pe[i].at(k, f"v{tb}"))
                dve.wait_ge(f_act[i].sem, f_act[i].at(k, f"th{tb}"))
                g = ffn_row[i][:, tb, :]
                dve.scalar_tensor_tensor(out=g, in0=g, scalar=1.0, in1=bank(f"f{i}v{tb}"), op0=ALU.add,
                                         op1=ALU.mult).then_inc(f_dve[i].sem, 1)

            def ffn_add(k, tb):
                dve.wait_ge(f_dve[0].sem, f_dve[0].at(k, f"g{tb}"))
                dve.tensor_tensor(xin[:, tb, :], ffn_row[0][:, tb, :], xin[:, tb, :],
                                  ALU.add).then_inc(f_dve[0].sem, 1)

            def mamba_inner(k):
                normalise(2, m_pool, m_dve, k, xin, ffn_row[0], TB)

            def mamba_outer(k, pair):
                if due(count := y_dve.at(k - 2, "x1")):
                    dve.wait_ge(y_dve.sem, count)
                normalise(2, m_pool, m_dve, k, xin, res[:, pair, :, :], 0)

            def conv_taps(k, j):
                for q in range(KC - 1):
                    for c in range(2):
                        et = 2 * j + c
                        if q == 0:
                            dve.wait_ge(m_act.sem, m_act.at(k, f"tap{'ab'[c]}{j}"))
                        else:
                            dve.wait_ge(m_dve.sem, m_dve.at(k, f"c{q - 1}{'ab'[c]}{j}"))
                        o = col3(xc2[:, et, :])
                        dve.scalar_tensor_tensor(out=o, in0=xs_pad[:, j % 2, c, :, q:q + T],
                                                 scalar=conv_sb[:, et, q:q + 1], in1=o, op0=ALU.mult,
                                                 op1=ALU.add).then_inc(m_dve.sem, 1)

            def conv_silu(k, j):
                dve.wait_ge(m_act.sem, m_act.at(k, f"th{j}"))
                o = xc2[:, 2 * j:2 * j + 2, :].rearrange("p c w -> p (c w)")
                dve.scalar_tensor_tensor(out=o, in0=ffn_row[0][:, j % 2, :], scalar=1.0, in1=o, op0=ALU.add,
                                         op1=ALU.mult).then_inc(m_dve.sem, 1)

            def softplus_sum(k, hf):
                dve.wait_ge(h_act.sem, h_act.at(k, f"ln{hf}"))
                d = delta[:, hf, :, :].rearrange("p e w -> p (e w)")
                dve.scalar_tensor_tensor(out=d, in0=d, scalar=0.0,
                                         in1=soft(hf), op0=ALU.max,
                                         op1=ALU.add).then_inc(h_dve.sem, 1)

            def gate_silu(k, j):
                dve.wait_ge(z_act.sem, z_act.at(k, f"{j}"))
                g = gate[:, 2 * j:2 * j + 2, :].rearrange("p c w -> p (c w)")
                dve.scalar_tensor_tensor(out=g, in0=g, scalar=1.0, in1=bank(f"z{j}"), op0=ALU.add,
                                         op1=ALU.mult).then_inc(z_dve.sem, 1)

            def gate_y(k, j):
                dve.wait_ge(y_pe.sem, y_pe.at(k, f"T{j}"))
                dve.wait_ge(z_dve.sem, z_dve.at(k, f"{j}"))
                if j < 2:
                    if due(count := f_pe[1].at(k - 1, "v1")):
                        dve.wait_ge(f_pe[1].sem, count)
                    o = ffn_col[1][:, 2 * j:2 * j + 2, 0:W]
                else:
                    if due(count := 2 * NSTEP * (k + 1)):
                        dve.wait_ge(dbx_done, count)
                    o = u[:, 1, 2 * j - HT:2 * j - HT + 2, :]
                dve.tensor_tensor(o, gate[:, 2 * j:2 * j + 2, :],
                                  bank(f"YT{j}").rearrange("p (c w) -> p c w", c=2),
                                  ALU.mult).then_inc(y_dve.sem, 1)

            def out_add(k, tb, pair):
                dve.wait_ge(y_pe.sem, y_pe.at(k, f"o{tb}"))
                dve.wait_ge(m_pool.sem, m_pool.at(k, "res"))
                if due(count := 16 * TB * k):
                    dve.wait_ge(out_stored, count)
                dve.scalar_tensor_tensor(out=xout[:, tb, :], in0=bank(f"o{tb}"), scalar=0.5,
                                         in1=res[:, pair, tb, :], op0=ALU.mult,
                                         op1=ALU.add).then_inc(y_dve.sem, 1)

            def scan(it, s):
                if due(count := 2 * NSTEP * it + 2 * s + 2):
                    dve.wait_ge(dbx_done, count)
                if due(count := NEXP * it + HT * (s + 1)):
                    dve.wait_ge(decay_done, count)
                hs = h[:, s % RING, :, :, :].rearrange("p e b s -> p (e b s)")
                dve.tensor_tensor_scan(hs, decay[:, s % 2, :, :, :].rearrange("p e b s -> p (e b s)"),
                                       hs, 0.0, ALU.mult, ALU.add).then_inc(scan_done, 1)

            def add_y(it, s, tb, pair):
                hf, n = divmod(s, NS)
                if due(count := NSTT * it + TB * s + tb + 1):
                    dve.wait_ge(h_turned, count)
                if n == 0:
                    dve.wait_ge(h_act.sem, h_act.at(it, f"yb{hf}"))
                else:
                    if due(count := NSTT * it + TB * (s - 1) + tb + 1):
                        dve.wait_ge(y_added, count)
                yy = y_rows[:, hf, tb, :]
                dve.scalar_tensor_tensor(out=yy, in0=h_rows[:, s % 2, tb, :],
                                         scalar=c_rows[:, pair, tb, n:n + 1],
                                         in1=yy, op0=ALU.mult, op1=ALU.add).then_inc(y_added, 1)

            def body(it, pair):
                scn, front, back, ahead = has(it, 0), has(it, 1), has(it, -1), has(it, 2)
                f, b = it + 1, it - 1
                other = (pair + 1) % PAIRS
                for s in range(NSTEP):
                    if scn:
                        scan(it, s)
                    for tb in range(TB):
                        if s < LAG:
                            if back:
                                add_y(b, NSTEP - LAG + s, tb, other)
                        elif scn:
                            add_y(it, s - LAG, tb, pair)
                    if back and s == 0:
                        gate_y(b, 0)
                        gate_y(b, 1)
                    if back and s == 1:
                        gate_silu(b, 3)
                    if front:
                        if s == 2:
                            ffn_mix_in(0, f, 1)
                        if s == 3:
                            ffn_mix_in(0, f, 0)
                    if scn and s == 3:
                        gate_silu(it, 0)
                    if scn and s == 15:
                        gate_silu(it, 1)
                    if back and s == 3:
                        gate_y(b, 2)
                        gate_y(b, 3)
                    if front:
                        if s == 9:
                            ffn_gate(0, f, 0)
                        if s == 9:
                            ffn_gate(0, f, 1)
                            ffn_add(f, 0)
                            ffn_add(f, 1)
                            dve.wait_ge(f_dve[0].sem, f_dve[0].at(f, "o1"))
                            if due(count := m_pool.at(f - 1, "v2")):
                                dve.wait_ge(m_pool.sem, count)
                            norm_stats(2, m_dve, f, xin)
                    if back and s == 11:
                        out_add(b, 0, other)
                    if scn and s == 11:
                        softplus_sum(it, 1)
                    if front and s == 11:
                        mamba_inner(f)
                    if back and s == 13:
                        out_add(b, 1, other)
                    if front and s == 13:
                        mamba_outer(f, other)
                    if back and s == 14:
                        dve.wait_ge(y_dve.sem, y_dve.at(b, "x1"))
                        ffn_stats(1, b, xout)
                    if front:
                        if s in (17, 18):
                            conv_taps(f, s - 17)
                        if s in (19, 20):
                            conv_silu(f, s - 19)
                        if s in (20, 21):
                            conv_taps(f, s - 18)
                    if back and s == 19:
                        ffn_mix_in(1, b, 1)
                    if front and s in (22, 23):
                        conv_silu(f, s - 20)
                    if back and s == 22:
                        ffn_mix_in(1, b, 0)
                    if scn and s == 21:
                        gate_silu(it, 2)
                    if ahead and s == 25:
                        dve.wait_ge(x_loaded, (it + 3) * (16 * TB))
                        ffn_stats(0, it + 2, xin)
                    if front and s == 29:
                        softplus_sum(f, 0)
                    if back:
                        if s in (29, 30):
                            ffn_gate(1, b, s - 29)

            run(body, dve)

        @block.gpsimd
        def _(pool):
            pool.memset(ident[:, :], 0.0).then_inc(init_pool, 1)
            pool.memset(wdt_sb[:, :], 0.0).then_inc(init_pool, 1)
            pool.wait_ge(init_pool, 1)
            pool.affine_select(out=ident[:, :], in_=ident[:, :], compare_op=ALU.not_equal, fill=1.0,
                               base=0, pattern=[[-1, P]], channel_multiplier=1).then_inc(init_pool, 1)
            pool.memset(xdbl[:, :], 0.0).then_inc(init_pool, 1)
            pool.memset(state[:, :, :, :, :], 0.0).then_inc(init_pool, 1)
            pool.memset(xs_last[:, :, :, :, :], 0.0).then_inc(init_pool, 1)
            for i in range(2):
                pool.memset(ffn_last[i][:, :, :, :], 0.0).then_inc(init_pool, 1)
            pool.memset(xscale[:, :], 0.5).then_inc(init_pool, 1)
            pool.wait_ge(init_pool, 9)
            pool.affine_select(out=xscale[:, :], in_=xscale[:, :], compare_op=ALU.is_gt, fill=0.25,
                               base=R, pattern=[[0, 1]], channel_multiplier=-1).then_inc(init_pool, 1)
            pool.wait_ge(init_pool, 10)
            pool.affine_select(out=xscale[:, :], in_=xscale[:, :], compare_op=ALU.is_gt, fill=0.5,
                               base=R + NS, pattern=[[0, 1]], channel_multiplier=-1).then_inc(init_pool, 1)
            pool.wait_ge(init_pool, 11)

            def rsqrt(q, marks, k, n):
                v, t, y = nv[q][:, 0:n], nt[q][:, 0:n], rs[q][:, 0:n]
                pool.wait_ge(marks.sem, marks.at(k, marks.names[marks.names.index("guess") - 1]))
                pool.sem_inc(passed_pool, 1)
                pool.tensor_scalar(y.bitcast(I32), v.bitcast(I32), -0.5, RSQRT_GUESS, ALU.mult,
                                   ALU.add).then_inc(marks.sem, 1)
                before = "guess"
                for i in range(NEWTON):
                    pool.wait_ge(marks.sem, marks.at(k, before))
                    pool.tensor_tensor(t, y, y, ALU.mult).then_inc(marks.sem, 1)
                    pool.wait_ge(marks.sem, marks.at(k, f"yy{i}"))
                    pool.tensor_tensor(t, t, v, ALU.mult).then_inc(marks.sem, 1)
                    pool.wait_ge(marks.sem, marks.at(k, f"vyy{i}"))
                    pool.sem_inc(passed_pool, 1)
                    pool.tensor_scalar(t, t, -0.5, 1.5, ALU.mult, ALU.add).then_inc(marks.sem, 1)
                    pool.wait_ge(marks.sem, marks.at(k, f"half{i}"))
                    pool.tensor_tensor(y, y, t, ALU.mult).then_inc(marks.sem, 1)
                    before = f"y{i}"

            def ffn_rstd(i, k):
                if due(count := f_act[i].at(k - 1, "ln1")):
                    pool.wait_ge(f_act[i].sem, count)
                pool.wait_ge(f_dve[i].sem, f_dve[i].at(k, "mv1"))
                pool.sem_inc(passed_pool, 1)
                pool.tensor_scalar(nv[i][:, 0:TB], mv[i][:, :, 1], 1.0, EPS, ALU.mult,
                                   ALU.add).then_inc(f_pool[i].sem, 1)
                rsqrt(i, f_pool[i], k, TB)
                pool.wait_ge(f_pool[i].sem, f_pool[i].at(k, f"y{NEWTON - 1}"))
                pool.tensor_tensor(shift[i][:, :], mv[i][:, :, 0], rs[i][:, 0:TB],
                                   ALU.mult).then_inc(f_pool[i].sem, 1)
                pool.wait_ge(f_pool[i].sem, f_pool[i].at(k, "mean"))
                pool.sem_inc(passed_pool, 1)
                pool.tensor_scalar(shift[i][:, :], shift[i][:, :], -1.0, 0.0, ALU.mult,
                                   ALU.add).then_inc(f_pool[i].sem, 1)

            def ffn_add(k):
                pool.wait_ge(f_dve[1].sem, f_dve[1].at(k, "g1"))
                pool.tensor_tensor(xout[:, :, :], xout[:, :, :], ffn_row[1][:, :, :],
                                   ALU.add).then_inc(f_pool[1].sem, 1)

            def mamba_rstd(k):
                if due(count := m_dve.at(k - 1, "ln1")):
                    pool.wait_ge(m_dve.sem, count)
                pool.wait_ge(m_dve.sem, m_dve.at(k, "mv1"))
                pool.sem_inc(passed_pool, 1)
                pool.tensor_scalar(nv[2][:, 0:TB], mv[2][:, :, 1], 1.0, EPS, ALU.mult,
                                   ALU.add).then_inc(m_pool.sem, 1)
                pool.tensor_scalar(nv[2][:, TB:2 * TB], mv[2][:, :, 1], 1.0 + EPS, EPS * EPS, ALU.mult,
                                   ALU.add).then_inc(m_pool.sem, 1)
                rsqrt(2, m_pool, k, 2 * TB)

            def make_res(k, pair):
                pool.wait_ge(m_dve.sem, m_dve.at(k, "ln1"))
                pool.tensor_tensor(res[:, pair, :, :], res[:, pair, :, :], xin[:, :, :], ALU.add).then_inc(m_pool.sem, 1)

            def make_u(k, hf):
                pool.wait_ge(h_dve.sem, h_dve.at(k, f"delta{hf}"))
                pool.wait_ge(m_dve.sem, m_dve.at(k, "silu3"))
                if hf == 1:
                    if due(count := y_pe.at(k - 1, "half1")):
                        pool.wait_ge(y_pe.sem, count)
                pool.tensor_tensor(u[:, hf, :, :], delta[:, hf, :, :], xc2[:, HT * hf:HT * (hf + 1), :],
                                   ALU.mult).then_inc(h_pool.sem, 1)

            def products(it, s, pair):
                hf, n = divmod(s, NS)
                if due(count := NSTT * it + TB * (s - RING + 1)):
                    pool.wait_ge(h_turned, count)
                    pool.sem_inc(passed_pool, 1)
                if due(count := NSTEP * it + s - RING + 1):
                    pool.wait_ge(saved, count)
                    pool.sem_inc(passed_pool, 1)
                pool.tensor_copy(h[:, s % RING, :, :, 0], state[:, pair, s, :, :]).then_inc(dbx_done, 1)
                j = s // NBG
                if s % NBG == 0:
                    pool.wait_ge(b_loaded[j % 2], it * (16 * NG // 2) + 16 * (j // 2 + 1))
                if n == 0:
                    pool.wait_ge(h_pool.sem, h_pool.at(it, f"u{hf}"))
                bb = b_all[:, j % 2, s % NBG, :].rearrange("p (b t) -> p b t", b=B)
                pool.tensor_tensor(h[:, s % RING, :, :, 1:SEG],
                                   u[:, hf, :, :].rearrange("p e (b t) -> p e b t", b=B),
                                   bb.unsqueeze(1).broadcast_to([P, HT, B, T]),
                                   ALU.mult).then_inc(dbx_done, 1)

            def body(it, pair):
                scn, front, back, ahead = has(it, 0), has(it, 1), has(it, -1), has(it, 2)
                f, b = it + 1, it - 1
                for s in range(NSTEP):
                    if scn:
                        products(it, s, pair)
                    if has(it, -2) and s == 2:
                        ffn_add(it - 2)
                    if front and s == 11:
                        mamba_rstd(f)
                    if scn and s == 15:
                        make_u(it, 1)
                    if back and s == 17:
                        ffn_rstd(1, b)
                    if front and s == 18:
                        make_res(f, (pair + 1) % PAIRS)
                    if ahead and s == 27:
                        ffn_rstd(0, it + 2)
                    if front and s == 31:
                        make_u(f, 0)

            run(body, pool)


def kernel(L0_attn_x, L0_attn_ln_w, L0_attn_ln_b, L0_attn_W_in, L0_attn_W_conv, L0_attn_b_conv,
           L0_attn_W_xproj, L0_attn_W_dt, L0_attn_b_dt, L0_attn_A_log, L0_attn_D_skip, L0_attn_W_out,
           L0_ffn_W_r, L0_ffn_W_k, L0_ffn_W_v, L0_ffn_mu_r, L0_ffn_mu_k):
    import numpy as np
    import concourse.bacc as bacc
    from concourse.bass_utils import run_bass_kernel_spmd

    def by_tile(v):
        return np.asarray(v).reshape(-1, P).T

    arrays = {
        "x": L0_attn_x, "mu_r": by_tile(L0_ffn_mu_r), "mu_k": by_tile(L0_ffn_mu_k),
        "w_r": np.asarray(L0_ffn_W_r).T, "w_k": np.asarray(L0_ffn_W_k).T,
        "w_v": np.asarray(L0_ffn_W_v).T, "ln_w": by_tile(L0_attn_ln_w), "ln_b": by_tile(L0_attn_ln_b),
        "w_in": np.asarray(L0_attn_W_in).T, "w_conv": L0_attn_W_conv, "b_conv": by_tile(L0_attn_b_conv),
        "w_x": np.asarray(L0_attn_W_xproj).T, "w_dt": np.asarray(L0_attn_W_dt).T,
        "b_dt": by_tile(L0_attn_b_dt), "a_log": L0_attn_A_log, "d_skip": by_tile(L0_attn_D_skip),
        "w_out": np.asarray(L0_attn_W_out).T,
    }
    arrays = {f"in_{n}": np.ascontiguousarray(a) for n, a in arrays.items()}
    nc = bacc.Bacc("TRN2", target_bir_lowering=False, num_devices=1)
    args = [nc.dram_tensor(n, a.shape, mybir.dt.from_np(a.dtype), kind="ExternalInput").ap()
            for n, a in arrays.items()]
    out = nc.dram_tensor("out_0", tuple(L0_attn_x.shape), F32, kind="ExternalOutput").ap()
    build(nc, *args, out)
    r = run_bass_kernel_spmd(nc, [arrays], core_ids=[0])
    return r.results[0]["out_0"]
```
